# Optimizing a Trainium2 kernel written in Bass

```python
import numpy as np
import jax
import jax.numpy as jnp

def _softmax(x, axis=-1):
    return jax.nn.softmax(x, axis=axis)

def _gelu(x):
    return jax.nn.gelu(x, approximate=True)

def _silu(x):
    return jax.nn.silu(x)

def _sigmoid(x):
    return jax.nn.sigmoid(x)

def _layernorm(x, axis=-1, eps=1e-05):
    m = jnp.mean(x, axis=axis, keepdims=True)
    v = jnp.var(x, axis=axis, keepdims=True)
    return (x - m) / jnp.sqrt(v + eps)

def _scatter_add(tgt, idx, src, axis=0):
    return tgt.at[idx].add(src)

def _segment_sum(src, seg, n):
    return jax.ops.segment_sum(src, seg, n)
kernel_name = 'mk_xattn_seq_d2_seqx_r4_b6f3cc'

def setup_inputs(seed: int=0):
    np.random.seed(seed)
    _w = jnp.asarray

    def _rec_inputs():
        import jax
        import jax.numpy as jnp
        _rk = jax.random.key(seed)
        x = 7.22e-05 + 1 * jax.random.normal(jax.random.fold_in(_rk, 1), (8, 512, 256), jnp.float32)
        _lenS = 512 - jax.random.randint(jax.random.fold_in(_rk, 7), (8,), 0, max(1, 512 // 4) + 1, jnp.int32)
        _lenS2 = 1601 - jax.random.randint(jax.random.fold_in(_rk, 8), (8,), 0, max(1, 1601 // 4) + 1, jnp.int32)
        _ctx_1024P = jax.random.normal(jax.random.fold_in(_rk, 11), (8, 16, 256), jnp.float32)
        _ctx_1024c = jax.random.dirichlet(jax.random.fold_in(_rk, 511), 0.3 * jnp.ones((16,), jnp.float32), (8, 1601))
        _ctx_1024t = jnp.einsum('bsk,bkd->bsd', _ctx_1024c, _ctx_1024P)
        _ctx_1024t = _ctx_1024t * jax.lax.rsqrt(jnp.mean(jnp.square(_ctx_1024t)) + 1e-12) * 0.953939
        ctx_1024 = 4.13588e-05 + 0.999923 * (_ctx_1024t + 0.3 * jax.random.normal(jax.random.fold_in(_rk, 611), (8, 1601, 256), jnp.float32))
        _validS = jnp.arange(512)[None, :] < _lenS[:, None]
        _validS2 = jnp.arange(1601)[None, :] < _lenS2[:, None]
        _causal = jnp.tril(jnp.ones((512, 512), dtype=bool))
        mask_SxS_fc0 = jnp.where(jnp.broadcast_to(_causal[:, :], (512, 512)), 0.0, -1000000000.0).astype(jnp.float32)
        return (x, ctx_1024, mask_SxS_fc0)
    x, ctx_1024, mask_SxS_fc0 = _rec_inputs()

    def _L0_xattn_setup():
        import jax, jax.numpy as jnp
        import numpy as np
        D_MODEL = 256
        NUM_HEADS = 16
        HEAD_DIM = D_MODEL // NUM_HEADS
        EPS = 1e-06

        def rmsnorm(x, w):
            xf = x.astype(jnp.float32)
            n = xf * jax.lax.rsqrt(jnp.mean(xf * xf, axis=-1, keepdims=True) + EPS)
            return (n * w.astype(jnp.float32)).astype(x.dtype)
        key = jax.random.key(seed)
        ks = jax.random.split(key, 8)
        B, S, K = (4, 512, 512)
        s = 1.0 / np.sqrt(D_MODEL)
        return {'x': jax.random.normal(ks[0], (B, S, D_MODEL), jnp.float32), 'kv': jax.random.normal(ks[1], (B, K, D_MODEL), jnp.float32), 'wq': jax.random.normal(ks[2], (D_MODEL, D_MODEL), jnp.float32) * s, 'wk': jax.random.normal(ks[3], (D_MODEL, D_MODEL), jnp.float32) * s, 'wv': jax.random.normal(ks[4], (D_MODEL, D_MODEL), jnp.float32) * s, 'wo': jax.random.normal(ks[5], (D_MODEL, D_MODEL), jnp.float32) * s, 'bo': jnp.zeros((D_MODEL,), jnp.float32), 'gq': jnp.ones((D_MODEL,), jnp.float32), 'gkv': jnp.ones((D_MODEL,), jnp.float32)}
    _L0_xattn_all = _L0_xattn_setup()
    _L0_xattn_in = {k: v for k, v in _L0_xattn_all.items() if k in ('wq', 'wk', 'wv', 'wo', 'bo', 'gq', 'gkv')}
    del _L0_xattn_all

    def _L1_xattn_setup():
        import jax, jax.numpy as jnp
        import numpy as np
        B, QL, KVL = (4, 256, 375)
        D, H, MLP = (256, 16, 1024)
        DH = D // H
        EPS = 1e-05
        NEG = -1000000000.0

        def layernorm(x, w, b):
            m = jnp.mean(x, axis=-1, keepdims=True)
            v = jnp.mean((x - m) ** 2, axis=-1, keepdims=True)
            return (x - m) / jnp.sqrt(v + EPS) * w + b

        def gelu_exact(x):
            return x * 0.5 * (1.0 + jax.lax.erf(x * np.float32(0.7071067811865476)))

        def mha(xq, xkv, qw, qb, kw, vw, vb, ow, ob, mask=None):
            nb, ql = (xq.shape[0], xq.shape[1])
            kl = xkv.shape[1]
            q = xq @ qw.T + qb
            k = xkv @ kw.T
            v = xkv @ vw.T + vb
            scale = np.float32(DH ** (-0.25))
            q = q.reshape(nb, ql, H, DH) * scale
            k = k.reshape(nb, kl, H, DH) * scale
            v = v.reshape(nb, kl, H, DH)
            logits = jnp.einsum('bqhd,bkhd->bhqk', q, k)
            if mask is not None:
                logits = logits + mask[:ql, :kl]
            p = jax.nn.softmax(logits, axis=-1)
            o = jnp.einsum('bhqk,bkhd->bqhd', p, v).reshape(nb, ql, H * DH)
            return o @ ow.T + ob
        key = jax.random.key(seed)
        ks = jax.random.split(key, 20)
        s = 0.02
        inp = {'x': jax.random.normal(ks[0], (B, QL, D), jnp.float32), 'xa': jax.random.normal(ks[1], (B, KVL, D), jnp.float32), 'mask': jnp.where(jnp.tril(jnp.ones((QL, QL), bool)), 0.0, NEG).astype(jnp.float32), 'attn_ln_w': jnp.ones((D,), jnp.float32), 'attn_ln_b': jnp.zeros((D,), jnp.float32), 'q_w': jax.random.normal(ks[2], (D, D), jnp.float32) * s, 'q_b': jnp.zeros((D,), jnp.float32), 'k_w': jax.random.normal(ks[3], (D, D), jnp.float32) * s, 'v_w': jax.random.normal(ks[4], (D, D), jnp.float32) * s, 'v_b': jnp.zeros((D,), jnp.float32), 'o_w': jax.random.normal(ks[5], (D, D), jnp.float32) * s, 'o_b': jnp.zeros((D,), jnp.float32), 'cross_ln_w': jnp.ones((D,), jnp.float32), 'cross_ln_b': jnp.zeros((D,), jnp.float32), 'cq_w': jax.random.normal(ks[6], (D, D), jnp.float32) * s, 'cq_b': jnp.zeros((D,), jnp.float32), 'ck_w': jax.random.normal(ks[7], (D, D), jnp.float32) * s, 'cv_w': jax.random.normal(ks[8], (D, D), jnp.float32) * s, 'cv_b': jnp.zeros((D,), jnp.float32), 'co_w': jax.random.normal(ks[9], (D, D), jnp.float32) * s, 'co_b': jnp.zeros((D,), jnp.float32), 'mlp_ln_w': jnp.ones((D,), jnp.float32), 'mlp_ln_b': jnp.zeros((D,), jnp.float32), 'fc1_w': jax.random.normal(ks[10], (MLP, D), jnp.float32) * s, 'fc1_b': jnp.zeros((MLP,), jnp.float32), 'fc2_w': jax.random.normal(ks[11], (D, MLP), jnp.float32) * s, 'fc2_b': jnp.zeros((D,), jnp.float32)}
        return inp
    _L1_xattn_all = _L1_xattn_setup()
    _L1_xattn_in = {k: v for k, v in _L1_xattn_all.items() if k in ('attn_ln_w', 'attn_ln_b', 'q_w', 'q_b', 'k_w', 'v_w', 'v_b', 'o_w', 'o_b', 'cross_ln_w', 'cross_ln_b', 'cq_w', 'cq_b', 'ck_w', 'cv_w', 'cv_b', 'co_w', 'co_b', 'mlp_ln_w', 'mlp_ln_b', 'fc1_w', 'fc1_b', 'fc2_w', 'fc2_b')}
    del _L1_xattn_all
    return {'x': x, 'ctx_1024': ctx_1024, 'mask_SxS_fc0': mask_SxS_fc0, 'L0_xattn_wq': _L0_xattn_in['wq'], 'L0_xattn_wk': _L0_xattn_in['wk'], 'L0_xattn_wv': _L0_xattn_in['wv'], 'L0_xattn_wo': _L0_xattn_in['wo'], 'L0_xattn_bo': _L0_xattn_in['bo'], 'L0_xattn_gq': _L0_xattn_in['gq'], 'L0_xattn_gkv': _L0_xattn_in['gkv'], 'L1_xattn_attn_ln_w': _L1_xattn_in['attn_ln_w'], 'L1_xattn_attn_ln_b': _L1_xattn_in['attn_ln_b'], 'L1_xattn_q_w': _L1_xattn_in['q_w'], 'L1_xattn_q_b': _L1_xattn_in['q_b'], 'L1_xattn_k_w': _L1_xattn_in['k_w'], 'L1_xattn_v_w': _L1_xattn_in['v_w'], 'L1_xattn_v_b': _L1_xattn_in['v_b'], 'L1_xattn_o_w': _L1_xattn_in['o_w'], 'L1_xattn_o_b': _L1_xattn_in['o_b'], 'L1_xattn_cross_ln_w': _L1_xattn_in['cross_ln_w'], 'L1_xattn_cross_ln_b': _L1_xattn_in['cross_ln_b'], 'L1_xattn_cq_w': _L1_xattn_in['cq_w'], 'L1_xattn_cq_b': _L1_xattn_in['cq_b'], 'L1_xattn_ck_w': _L1_xattn_in['ck_w'], 'L1_xattn_cv_w': _L1_xattn_in['cv_w'], 'L1_xattn_cv_b': _L1_xattn_in['cv_b'], 'L1_xattn_co_w': _L1_xattn_in['co_w'], 'L1_xattn_co_b': _L1_xattn_in['co_b'], 'L1_xattn_mlp_ln_w': _L1_xattn_in['mlp_ln_w'], 'L1_xattn_mlp_ln_b': _L1_xattn_in['mlp_ln_b'], 'L1_xattn_fc1_w': _L1_xattn_in['fc1_w'], 'L1_xattn_fc1_b': _L1_xattn_in['fc1_b'], 'L1_xattn_fc2_w': _L1_xattn_in['fc2_w'], 'L1_xattn_fc2_b': _L1_xattn_in['fc2_b']}

def reference(x, ctx_1024, mask_SxS_fc0, L0_xattn_wq, L0_xattn_wk, L0_xattn_wv, L0_xattn_wo, L0_xattn_bo, L0_xattn_gq, L0_xattn_gkv, L1_xattn_attn_ln_w, L1_xattn_attn_ln_b, L1_xattn_q_w, L1_xattn_q_b, L1_xattn_k_w, L1_xattn_v_w, L1_xattn_v_b, L1_xattn_o_w, L1_xattn_o_b, L1_xattn_cross_ln_w, L1_xattn_cross_ln_b, L1_xattn_cq_w, L1_xattn_cq_b, L1_xattn_ck_w, L1_xattn_cv_w, L1_xattn_cv_b, L1_xattn_co_w, L1_xattn_co_b, L1_xattn_mlp_ln_w, L1_xattn_mlp_ln_b, L1_xattn_fc1_w, L1_xattn_fc1_b, L1_xattn_fc2_w, L1_xattn_fc2_b):
    import jax
    import jax.numpy as jnp

    def _L0_xattn_ref(x, kv, wq, wk, wv, wo, bo, gq, gkv):
        import jax, jax.numpy as jnp
        import numpy as np
        D_MODEL = 256
        NUM_HEADS = 16
        HEAD_DIM = D_MODEL // NUM_HEADS
        EPS = 1e-06

        def rmsnorm(x, w):
            xf = x.astype(jnp.float32)
            n = xf * jax.lax.rsqrt(jnp.mean(xf * xf, axis=-1, keepdims=True) + EPS)
            return (n * w.astype(jnp.float32)).astype(x.dtype)
        B, S, _ = x.shape
        K = kv.shape[1]
        xn = rmsnorm(x, gq)
        kvn = rmsnorm(kv, gkv)
        q = (xn @ wq.T).reshape(B, S, NUM_HEADS, HEAD_DIM)
        k = (kvn @ wk.T).reshape(B, K, NUM_HEADS, HEAD_DIM)
        v = (kvn @ wv.T).reshape(B, K, NUM_HEADS, HEAD_DIM)
        scale = HEAD_DIM ** (-0.5)
        scores = jnp.einsum('bshd,bkhd->bhsk', q, k) * scale
        attn = jax.nn.softmax(scores, axis=-1)
        o = jnp.einsum('bhsk,bkhd->bshd', attn, v).reshape(B, S, D_MODEL)
        out = o @ wo.T + bo
        return xn + out

    def _L1_xattn_ref(x, xa, mask, attn_ln_w, attn_ln_b, q_w, q_b, k_w, v_w, v_b, o_w, o_b, cross_ln_w, cross_ln_b, cq_w, cq_b, ck_w, cv_w, cv_b, co_w, co_b, mlp_ln_w, mlp_ln_b, fc1_w, fc1_b, fc2_w, fc2_b):
        import jax, jax.numpy as jnp
        import numpy as np
        B, QL, KVL = (4, 256, 375)
        D, H, MLP = (256, 16, 1024)
        DH = D // H
        EPS = 1e-05
        NEG = -1000000000.0

        def layernorm(x, w, b):
            m = jnp.mean(x, axis=-1, keepdims=True)
            v = jnp.mean((x - m) ** 2, axis=-1, keepdims=True)
            return (x - m) / jnp.sqrt(v + EPS) * w + b

        def gelu_exact(x):
            return x * 0.5 * (1.0 + jax.lax.erf(x * np.float32(0.7071067811865476)))

        def mha(xq, xkv, qw, qb, kw, vw, vb, ow, ob, mask=None):
            nb, ql = (xq.shape[0], xq.shape[1])
            kl = xkv.shape[1]
            q = xq @ qw.T + qb
            k = xkv @ kw.T
            v = xkv @ vw.T + vb
            scale = np.float32(DH ** (-0.25))
            q = q.reshape(nb, ql, H, DH) * scale
            k = k.reshape(nb, kl, H, DH) * scale
            v = v.reshape(nb, kl, H, DH)
            logits = jnp.einsum('bqhd,bkhd->bhqk', q, k)
            if mask is not None:
                logits = logits + mask[:ql, :kl]
            p = jax.nn.softmax(logits, axis=-1)
            o = jnp.einsum('bhqk,bkhd->bqhd', p, v).reshape(nb, ql, H * DH)
            return o @ ow.T + ob
        h = layernorm(x, attn_ln_w, attn_ln_b)
        x = x + mha(h, h, q_w, q_b, k_w, v_w, v_b, o_w, o_b, mask=mask)
        h = layernorm(x, cross_ln_w, cross_ln_b)
        x = x + mha(h, xa, cq_w, cq_b, ck_w, cv_w, cv_b, co_w, co_b, mask=None)
        h = layernorm(x, mlp_ln_w, mlp_ln_b)
        h = gelu_exact(h @ fc1_w.T + fc1_b)
        x = x + (h @ fc2_w.T + fc2_b)
        return x
    x = _L0_xattn_ref(x, ctx_1024, L0_xattn_wq, L0_xattn_wk, L0_xattn_wv, L0_xattn_wo, L0_xattn_bo, L0_xattn_gq, L0_xattn_gkv)
    x = _L1_xattn_ref(x, ctx_1024, mask_SxS_fc0, L1_xattn_attn_ln_w, L1_xattn_attn_ln_b, L1_xattn_q_w, L1_xattn_q_b, L1_xattn_k_w, L1_xattn_v_w, L1_xattn_v_b, L1_xattn_o_w, L1_xattn_o_b, L1_xattn_cross_ln_w, L1_xattn_cross_ln_b, L1_xattn_cq_w, L1_xattn_cq_b, L1_xattn_ck_w, L1_xattn_cv_w, L1_xattn_cv_b, L1_xattn_co_w, L1_xattn_co_b, L1_xattn_mlp_ln_w, L1_xattn_mlp_ln_b, L1_xattn_fc1_w, L1_xattn_fc1_b, L1_xattn_fc2_w, L1_xattn_fc2_b)
    return x

_drawn_inputs = setup_inputs


def setup_inputs(seed=0):
    import zlib

    import numpy as np

    out = dict(_drawn_inputs(seed))
    spreads = {'L0_xattn_bo': (0.0, 0.1),
     'L0_xattn_gq': (1.0, 0.2),
     'L0_xattn_gkv': (1.0, 0.2),
     'L1_xattn_attn_ln_w': (1.0, 0.6),
     'L1_xattn_attn_ln_b': (0.0, 0.8),
     'L1_xattn_q_b': (0.0, 0.8),
     'L1_xattn_v_b': (0.0, 0.315),
     'L1_xattn_o_b': (0.0, 0.1),
     'L1_xattn_cross_ln_w': (1.0, 0.6),
     'L1_xattn_cross_ln_b': (0.0, 0.8),
     'L1_xattn_cq_b': (0.0, 0.8),
     'L1_xattn_cv_b': (0.0, 0.317),
     'L1_xattn_co_b': (0.0, 0.1),
     'L1_xattn_mlp_ln_w': (1.0, 0.6),
     'L1_xattn_mlp_ln_b': (0.0, 0.8),
     'L1_xattn_fc1_b': (0.0, 0.1),
     'L1_xattn_fc2_b': (0.0, 0.1)}
    factors = {'mask_SxS_fc0': 6.84,
     'L1_xattn_q_w': 8.0,
     'L1_xattn_k_w': 8.0,
     'L1_xattn_cq_w': 8.0,
     'L1_xattn_ck_w': 8.0}
    for name, (base, spread) in spreads.items():
        noise = np.random.default_rng([zlib.crc32(name.encode()), seed]).standard_normal(out[name].shape)
        drawn = base * np.exp(spread * noise) if base else spread * noise
        out[name] = jnp.asarray(drawn.astype(out[name].dtype))
    for name, factor in factors.items():
        out[name] = (out[name] * factor).astype(out[name].dtype)
    return out
```

```python
from contextlib import ExitStack

import concourse.bass as bass
import concourse.mybir as mybir

P = 128
B, S, D = 8, 512, 256
H, DH = 16, 16
KV = 1601
F = 1024
GH = 4
NG = H // GH
GW = GH * DH
VH = DH + 1
DC = D // P
FC = F // P
NQT = S // P
KVT = -(-KV // P)
SCALE = DH ** -0.5
EPS_RMS, EPS_LN = 1e-6, 1e-5
K_PARTS = [0, 0, 0, 1, 1, 2]
Q_PARTS = [0, 1, 2, 0, 1, 0]
PR = DH * len(K_PARTS)
MR = 2
NP = 3
FLAT = GH * NG * KV

ROW_NAMES = ["L0_xattn_gq", "L0_xattn_bo", "L1_xattn_v_b", "L1_xattn_o_b",
             "L1_xattn_cv_b", "L1_xattn_co_b", "L1_xattn_fc2_b"]
COL_NAMES = ["L0_xattn_gq", "L0_xattn_gkv", "L1_xattn_attn_ln_w", "L1_xattn_attn_ln_b",
             "L1_xattn_cross_ln_w", "L1_xattn_cross_ln_b", "L1_xattn_mlp_ln_w", "L1_xattn_mlp_ln_b",
             "L1_xattn_q_b", "L1_xattn_cq_b", "L1_xattn_fc1_b"]

LOWEST = -3.4028234e38
BF16_ONES = 1.0019379

F32 = mybir.dt.float32
BF16 = mybir.dt.bfloat16
ALU = mybir.AluOpType
ACT = mybir.ActivationFunctionType
AX = mybir.AxisListType


class Count:

    def __init__(self, sems, unit=1, start=1):
        self.sems, self.unit = sems, unit
        self.base, self.per = {}, {}
        self.total = [start] * len(sems)

    def plan(self, stage, uses, times=B):
        n = len(self.sems)
        self.base[stage] = list(self.total)
        self.per[stage] = [len(range(s, uses, n)) for s in range(n)]
        self.total = [t + times * p for t, p in zip(self.total, self.per[stage])]

    def sem(self, k):
        return self.sems[k % len(self.sems)]

    def before(self, stage, b, k):
        s = k % len(self.sems)
        fixed = (self.base[stage][s] + k // len(self.sems)) * self.unit
        return self.sems[s], b * (self.per[stage][s] * self.unit) + fixed

    def done(self, stage, b, k):
        sem, value = self.before(stage, b, k)
        return sem, value + self.unit


class Stage:

    def __init__(self, name, index, keys, masked):
        self.name, self.index, self.keys, self.masked = name, index, keys, masked
        self.KT = -(-keys // P)
        self.NCH = -(-keys // 512)
        width = -(-keys // self.NCH)
        self.chunks = [(c * width, min(width, keys - c * width)) for c in range(self.NCH)]
        self.rows = [min(P, keys - t * P) for t in range(self.KT)]
        self.ROWS = GH * NQT
        self.share = [[r for r in range(self.ROWS) if r * (self.KT - 1) // self.ROWS == t] for t in range(self.KT)]
        tail = ["oT0", "oT1", "out0", "out1", "hT0", "hT1"]
        if name == "L0":
            tail += ["q0", "q1", "k0", "k1", "v0", "v1"]
        if name == "self":
            tail += ["q0", "q1"]
        self.small = []
        for g in range(NG):
            if g:
                self.small.append(f"turn{g - 1}")
            self.small.append(f"max{g}")
        self.small += [f"turn{NG - 1}"] + tail

    def small_use(self, what, last):
        at = self.small.index(what)
        return 1 + at - (last and at > self.small.index(f"max{NG - 1}"))


L0, SELF, CROSS = Stage("L0", 0, KV, False), Stage("self", 1, S, True), Stage("cross", 2, KV, False)
STAGES = (L0, SELF, CROSS)


def build(nc, a, out):
    ctx = ExitStack()
    with ctx:
        def sb(name, shape, dt=F32):
            return ctx.enter_context(nc.sbuf_tensor(name, shape, dt))

        counts = []

        def sems(name, n=1, unit=1):
            counts.append(Count([ctx.enter_context(nc.semaphore(f"{name}{i}" if n > 1 else name)) for i in range(n)], unit))
            return counts[-1]

        def sem(name):
            return ctx.enter_context(nc.semaphore(name))

        def dram(name, shape, dt=F32):
            return nc.dram_tensor(name, shape, dt).ap()

        k_dram = [dram(f"k_parts_{s.name}", (B, 3, D, s.keys), BF16) for s in STAGES]
        q_dram = [dram(f"q_parts_{s.name}", (B, 3, D, S), BF16) for s in STAGES]
        v_dram = [dram(f"v_{s.name}", (B, NG, P, s.KT * GH * VH)) for s in STAGES]
        x_dram = [dram(f"x_{i}", (B, S, D)) for i in range(4)]
        h_dram = dram("h_mlp", (B, P, DC * S))

        keys_flat = sb("keys_flat", [P, FLAT], BF16)
        keys = keys_flat[:, :].rearrange("p (g j t) -> p g j t", g=NG, j=GH)
        queries = sb("queries", [P, NG, GH, S], BF16)
        values = sb("values", [P, NG, KVT, GH, VH])
        probs = sb("probs", [P, NP, GH * S])
        v_stage = sb("v_stage", [P, NG, KVT, GH, VH])
        w_names = ["L0_xattn_wq", "L0_xattn_wk", "L0_xattn_wv", "L0_xattn_wo",
                   "L1_xattn_q_w", "L1_xattn_k_w", "L1_xattn_v_w", "L1_xattn_o_w",
                   "L1_xattn_cq_w", "L1_xattn_ck_w", "L1_xattn_cv_w", "L1_xattn_co_w"]
        weights = sb("weights", [P, len(w_names), DC, D])
        w = {n: weights[:, i] for i, n in enumerate(w_names)}
        mask_q = sb("mask_q", [P, NQT, S])
        mask_k = sb("mask_k", [P, S // P, S])
        x_res = sb("x_res", [P, NQT, D])
        x_new = sb("x_new", [P, NQT, D])
        x_hat = sb("x_hat", [P, NQT, D])
        hT = sb("hT", [P, DC, S])
        o_tok = sb("o_tok", [P, NQT, D])
        oT = sb("oT", [P, DC, S])
        o_sum = sb("o_sum", [P, S])
        proj = sb("proj", [P, 2, S])
        parts = sb("parts", [P, 2, 3, S], BF16)
        rows = sb("rows", [P, len(ROW_NAMES), D])
        row = {n: rows[:, i] for i, n in enumerate(ROW_NAMES)}
        cols = sb("cols", [P, len(COL_NAMES), DC])
        col = {n: cols[:, i] for i, n in enumerate(COL_NAMES[:-1])}
        fc1_b = sb("fc1_b", [P, FC])
        q_bias = sb("q_bias", [P, 2, DC])
        ident = sb("ident", [P, P])
        ident_b = sb("ident_b", [P, P], BF16)
        neg_half = sb("neg_half", [P, KVT + NQT])
        NTT = KVT + NQT
        stats = sb("stats", [P, NTT, 6])
        mean_var = sb("mean_var", [P, NTT, 2])
        spread = sb("spread", [P, 2, NTT])
        rstd = sb("rstd", [P, NTT])
        part_max = sb("part_max", [P, GH * NQT * 4])
        neg_max = sb("neg_max", [P, GH * NQT])
        max_parts = sb("max_parts", [P, MR * GH * NQT], BF16)
        max_rows = sb("max_rows", [MR * GH * NQT, P], BF16)
        junk = sb("junk", [P, 2, S], BF16)
        recip = sb("recip", [P, NQT, GH])

        f32_flat = keys_flat[:, :].bitcast(F32)
        c_tok = f32_flat[:, 0:KVT * D].rearrange("p (t d) -> p t d", t=KVT)
        at = KVT * D
        c_raw = f32_flat[:, at:at + DC * KV].rearrange("p (c t) -> p c t", c=DC)
        at += DC * KV
        c_norm = f32_flat[:, at:at + DC * KV].rearrange("p (c t) -> p c t", c=DC)
        fc1 = f32_flat[:, 0:DC * F].rearrange("p (c f) -> p c f", c=DC)
        fc2 = f32_flat[:, DC * F:DC * F + FC * D].rearrange("p (c d) -> p c d", c=FC)
        at = DC * F + FC * D
        h1 = f32_flat[:, at:at + 2 * FC * S // 2].rearrange("p (i c t) -> p i c t", i=1, c=FC)

        psum = ctx.enter_context(nc.psum_tensor("psum", [P, 8, 512], F32))
        s_ps = psum[:, 0:4].rearrange("p (u j) t -> p u j t", u=2)
        m_ps = psum[:, 4:6]
        o_ps = psum[:, 6]
        small = psum[:, 7]

        def tok(dr, b):
            return dr[bass.ds(b, 1)].rearrange("b (t p) d -> p (b t) d", p=P)

        def staged(t, r=P):
            return v_stage[0:r, :, t, :, 0:DH]

        def by_head(ap):
            return ap.rearrange("p (g j d) -> p g j d", g=NG, j=GH)

        constants = sem("constants_loaded")
        ctx_loaded = sems("ctx_tokens_loaded", unit=16)
        raw_loaded = sems("ctx_raw_loaded", unit=16)
        xin_loaded = sems("x_loaded", unit=16)
        ident_made = sem("ident_made")
        bias_made = sem("bias_made")
        consts_set = sem("consts_set")
        norm_step = sems("norm_step")
        rstd_made = sems("rstd_made")
        hat_made = sems("hat_made")
        big_full = sems("bank_full", 8)
        turned = sems("turned")
        proj_made = sems("proj_made", 2)
        rest_step = sems("rest_step", 2)
        rest_made = sems("rest_made", 2)
        parts_made = sems("parts_made", 2)
        parts_stored = sems("parts_stored", 2, 16)
        v_made = sems("v_made")
        v_stored = sems("v_stored", unit=16)
        xn_made = sems("xn_made")
        xn_stored = sems("xn_stored", unit=16)

        N_LOADS = len(K_PARTS) + len(Q_PARTS) + 1
        group_loaded = sems("group_loaded", NG, 16 * N_LOADS)
        max_rows_loaded = sems("max_rows_loaded", NG, 16 * MR)
        ones_set = sem("ones_set")
        s_full = sems("scores_ready", 2)
        masked_done = sems("masked", 2)
        exp_done = sems("exp_done", 2)
        pv_done = sems("weighted_sum_added", NP)
        m_full = sems("max_scores_ready", 2)
        m_free = sems("max_taken", 2)
        max_step = sems("max_negated")
        max_first = sems("max_first_part")
        max_rest = sems("max_rest")
        max_ready = sems("max_parts_ready")
        small_full = sems("small_bank_full")
        small_free = sems("small_bank_read")
        o_moved = sems("sums_in_sbuf")
        recip_made = sems("reciprocal_made")
        res_loaded = sems("residual_loaded", unit=16)
        res_made = sems("residual_made")
        x_stored = sems("x_stored", unit=16)
        t_step = sems("tail_norm_step")
        t_rstd = sems("tail_rstd_made")
        t_hat = sems("tail_hat_made")
        h_stored = sems("h_stored", unit=16)

        fc_loaded = sem("fc_weights_loaded")
        h_loaded = sems("h_loaded", unit=16)
        f_full = sems("fc_bank_full", 8)
        gelu_done = sems("gelu_done")
        y_made = sems("y_made")
        waited = {"dve": sem("vector_waited"), "sp": sem("sync_waited")}

        with nc.Block() as block:
            @block.sync
            def _(sp):
                for c in counts:
                    for one in c.sems:
                        sp.sem_inc(one, c.unit)

        def settle(eng, name):
            eng.sem_inc(waited[name], 1)

        kv_jobs = [(L0, w["L0_xattn_wk"], w["L0_xattn_wv"], c_norm, None),
                   (CROSS, w["L1_xattn_ck_w"], w["L1_xattn_cv_w"], c_raw, row["L1_xattn_cv_b"])]
        t_groups = [list(range(i, min(i + 4, KVT))) for i in range(0, KVT, 4)]
        v_pairs = [list(range(i, min(i + 2, KVT))) for i in range(0, KVT, 2)]
        plan = [("turn", c, ts) for c in range(DC) for ts in t_groups]
        plan += [("xturn", c, None) for c in range(DC)]
        splits = []
        for n in range(2):
            for o in range(DC):
                for ch in L0.chunks:
                    splits.append((n, o, ch))
                    plan.append(("key", n, (o, ch)))
            plan += [("value", n, ts) for ts in v_pairs]
            if n == 0:
                for o in range(DC):
                    splits.append(("q", o, (0, S)))
                    plan.append(("query", o, None))
        n_turn = sum(p[0] in ("turn", "xturn") for p in plan)
        n_v = len(v_pairs)
        for c, uses in ((ctx_loaded, 2), (raw_loaded, 1), (xin_loaded, 1), (norm_step, 4), (rstd_made, 1),
                        (hat_made, NTT), (big_full, len(plan)), (turned, n_turn),
                        (proj_made, len(splits)), (rest_step, len(splits)), (rest_made, len(splits)), (parts_made, len(splits)),
                        (parts_stored, len(splits)), (v_made, 2 * n_v), (v_stored, 2), (xn_made, 1), (xn_stored, 1)):
            c.plan("context", uses)
        A = "context"
        n_const = len(w_names) + len(ROW_NAMES) + len(COL_NAMES) + 2
        reader, u, v, t = [], 0, 0, 0
        for kind, _, _ in plan:
            if kind in ("turn", "xturn"):
                reader.append((turned, t))
                t += 1
            elif kind == "value":
                reader.append((v_made, v))
                v += 1
            else:
                reader.append((proj_made, u))
                u += 1

        with nc.Block() as block:
            @block.sync
            def _(sp):
                def load_tokens(b):
                    full = (KVT - 1) * P
                    src = a["ctx"][bass.ds(b, 1), 0:full, :].rearrange("b (t p) d -> p (b t) d", p=P)
                    sp.dma_start(c_tok[:, 0:KVT - 1, :], src).then_inc(ctx_loaded.sem(0), 16)
                    rest = a["ctx"][bass.ds(b, 1), full:KV, :].rearrange("b p d -> p (b d)")
                    sp.dma_start(c_tok[0:KV - full, KVT - 1, :], rest).then_inc(ctx_loaded.sem(0), 16)
                    sp.dma_start(x_res[:, :, :], tok(a["x"], b)).then_inc(xin_loaded.sem(0), 16)

                def load_raw(b):
                    src = a["ctx_T"][bass.ds(b, 1)].rearrange("b (c p) t -> p (b c) t", p=P)
                    sp.dma_start(c_raw, src).then_inc(raw_loaded.sem(0), 16)

                load_tokens(0)
                for n in w_names:
                    sp.dma_start(w[n], a[n].rearrange("(c p) o -> p c o", p=P)).then_inc(constants, 16)
                for n in ROW_NAMES:
                    sp.dma_start(row[n], a[n].rearrange("(a d) -> a d", a=1).broadcast_to([P, D])).then_inc(constants, 16)
                for n in COL_NAMES[:-1]:
                    sp.dma_start(col[n], a[n + "_col"]).then_inc(constants, 16)
                sp.dma_start(fc1_b[:, :], a["L1_xattn_fc1_b_col"]).then_inc(constants, 16)
                sp.dma_start(mask_q[:, :, :], a["mask"].rearrange("(t p) k -> p t k", p=P)).then_inc(constants, 16)
                sp.dma_start(mask_k[:, :, :], a["mask_T"].rearrange("(t p) q -> p t q", p=P)).then_inc(constants, 16)
                load_raw(0)

                def stores(b, last):
                    u = 0
                    for kind, n, what in plan:
                        if kind == "xturn" and n == DC - 1:
                            sp.wait_ge(*xn_made.done(A, b, 0))
                            sp.dma_start(tok(x_dram[0], b), x_new[:, :, :]).then_inc(xn_stored.sem(0), 16)
                            if not last:
                                sp.wait_ge(*turned.done(A, b, n_turn - 1))
                                load_tokens(b + 1)
                        if kind in ("key", "query"):
                            sp.wait_ge(*parts_made.done(A, b, u))
                            settle(sp, "sp")
                            j, o, (c0, cw) = splits[u]
                            dst = q_dram[0] if j == "q" else k_dram[kv_jobs[j][0].index]
                            dst = dst[bass.ds(b, 1), :, o * P:(o + 1) * P, c0:c0 + cw].rearrange("b a p t -> p (b a) t")
                            sp.dma_start(dst, parts[:, u % 2, :, 0:cw]).then_inc(parts_stored.sem(u), 16)
                            u += 1
                        if kind == "value" and what is v_pairs[-1]:
                            sp.wait_ge(*v_made.done(A, b, (n + 1) * n_v - 1))
                            dst = v_dram[kv_jobs[n][0].index][bass.ds(b, 1)].rearrange("b g p e -> p (b g) e")
                            sp.dma_start(dst, v_stage[:, :].rearrange("p g t j e -> p g (t j e)")).then_inc(v_stored.sem(0), 16)
                    if not last:
                        sp.wait_ge(*big_full.done(A, b, len(plan) - 1))
                        load_raw(b + 1)

                with sp.Fori(0, B - 1) as b:
                    stores(b, False)
                stores(B - 1, True)
                sp.wait_ge(*xn_stored.done(A, B - 1, 0))
                sp.wait_ge(*v_stored.done(A, B - 1, 1))
                for u in (len(splits) - 2, len(splits) - 1):
                    sp.wait_ge(*parts_stored.done(A, B - 1, u))

            @block.gpsimd
            def _(pool):
                nc.gpsimd.memset(ident[:, :], 0.0).then_inc(ident_made, 1)
                nc.gpsimd.memset(ident_b[:, :], 0.0).then_inc(ident_made, 1)
                pool.wait_ge(ident_made, 2)
                for m in (ident, ident_b):
                    nc.gpsimd.affine_select(out=m[:, :], in_=m[:, :], compare_op=ALU.not_equal, fill=1.0, base=0,
                                            pattern=[[-1, P]], channel_multiplier=1).then_inc(ident_made, 1)
                nc.gpsimd.memset(neg_half[:, :], -0.5).then_inc(consts_set, 1)
                nc.gpsimd.memset(v_stage[:, :], 1.0).then_inc(consts_set, 1)
                pool.wait_ge(constants, 16 * n_const)

                with pool.Fori(0, B) as b:
                    pool.wait_ge(*norm_step.done(A, b, 3))
                    nc.gpsimd.tensor_tensor(rstd[:, :], spread[:, 1, :], neg_half[:, :], ALU.pow).then_inc(rstd_made.sem(0), 1)
                    u = 0
                    for kind, n, _ in plan:
                        if kind == "xturn" and n == 0:
                            pool.wait_ge(*hat_made.done(A, b, NTT - 1))
                            pool.wait_ge(*xn_stored.before(A, b, 0))
                            nc.gpsimd.tensor_tensor(x_new[:, :, :], x_hat[:, :, :],
                                                    row["L0_xattn_gq"].unsqueeze(1).broadcast_to([P, NQT, D]),
                                                    ALU.mult).then_inc(xn_made.sem(0), 1)
                        if kind in ("key", "query"):
                            cw = splits[u][2][1]
                            pool.wait_ge(*rest_made.done(A, b, u))
                            nc.gpsimd.tensor_tensor(parts[:, u % 2, 2, 0:cw], proj[:, u % 2, 0:cw], parts[:, u % 2, 1, 0:cw],
                                                    ALU.subtract).then_inc(parts_made.sem(u), 1)
                            u += 1

            @block.vector
            def _(dve):
                nc.vector.memset(mean_var[:, :, :], 1.0).then_inc(bias_made, 1)
                dve.wait_ge(constants, 16 * n_const)
                for i, n in enumerate(("L1_xattn_q_b", "L1_xattn_cq_b")):
                    nc.vector.tensor_scalar(q_bias[:, i, :], col[n], SCALE, None, ALU.mult).then_inc(bias_made, 1)
                nc.vector.memset(o_ps, 0.0).then_inc(bias_made, 1)
                dve.wait_ge(bias_made, 4)
                dve.wait_ge(consts_set, 2)

                with dve.Fori(0, B) as b:
                    tiles = [(t, c_tok[0:L0.rows[t], t, :], L0.rows[t]) for t in range(KVT)]
                    tiles += [(KVT + t, x_res[:, t, :], P) for t in range(NQT)]
                    dve.wait_ge(*ctx_loaded.done(A, b, 1))
                    dve.wait_ge(*xin_loaded.done(A, b, 0))
                    for t, src, r in tiles:
                        last = nc.vector.bn_stats(stats[0:r, t, :], src)
                    last.then_inc(norm_step.sem(0), 1)
                    dve.wait_ge(*norm_step.done(A, b, 0))
                    settle(dve, "dve")
                    for t, src, r in tiles:
                        last = nc.vector.bn_aggr(mean_var[0:r, t, :], stats[0:r, t, :])
                    last.then_inc(norm_step.sem(0), 1)
                    dve.wait_ge(*norm_step.done(A, b, 1))
                    nc.vector.tensor_tensor(spread[:, 0, :], mean_var[:, :, 0], mean_var[:, :, 0], ALU.mult).then_inc(norm_step.sem(0), 1)
                    dve.wait_ge(*norm_step.done(A, b, 2))
                    nc.vector.scalar_tensor_tensor(out=spread[:, 1, :], in0=spread[:, 0, :], scalar=EPS_RMS, in1=mean_var[:, :, 1],
                                                   op0=ALU.add, op1=ALU.add).then_inc(norm_step.sem(0), 1)
                    dve.wait_ge(*rstd_made.done(A, b, 0))
                    dve.wait_ge(*xn_made.before(A, b, 0))
                    dve.wait_ge(*turned.before(A, b, 0))
                    for t, src, r in tiles:
                        dst = src if t < KVT else x_hat[:, t - KVT, :]
                        nc.vector.tensor_scalar(dst, src, rstd[0:r, t:t + 1], None, ALU.mult).then_inc(hat_made.sem(0), 1)
                    u = 0
                    for k, (kind, n, what) in enumerate(plan):
                        if kind in ("key", "query"):
                            cw = splits[u][2][1]
                            f, p = proj[:, u % 2, 0:cw], parts[:, u % 2, :, 0:cw]
                            dve.wait_ge(*proj_made.done(A, b, u))
                            nc.vector.tensor_tensor(f, f, p[:, 0, :], ALU.subtract).then_inc(rest_step.sem(u), 1)
                            dve.wait_ge(*rest_step.done(A, b, u))
                            nc.vector.tensor_copy(p[:, 1, :], f).then_inc(rest_made.sem(u), 1)
                            u += 1
                        if kind == "value":
                            bias = kv_jobs[n][4]
                            dve.wait_ge(*big_full.done(A, b, k))
                            if what is v_pairs[0]:
                                dve.wait_ge(*v_stored.before(A, b, n))
                            for i, t in enumerate(what):
                                r = L0.rows[t]
                                dst = staged(t, r)
                                src = by_head(psum[0:r, k % 8, i * D:(i + 1) * D])
                                if bias is None:
                                    last = nc.vector.tensor_copy(dst, src)
                                else:
                                    last = nc.vector.tensor_tensor(dst, src, by_head(bias[0:r]), ALU.add)
                                if i + 1 < len(what):
                                    continue
                                last.then_inc(v_made.sem(0), 1)

            @block.scalar
            def _(act):
                act.wait_ge(constants, 16 * n_const)
                with act.Fori(0, B) as b:
                    u = 0
                    for k, (kind, n, what) in enumerate(plan):
                        bank = psum[:, k % 8]
                        if kind in ("turn", "xturn"):
                            act.wait_ge(*big_full.done(A, b, k))
                        if kind == "turn":
                            t0, t1 = what[0] * P, min(what[-1] * P + P, KV)
                            nc.scalar.activation(c_norm[:, n, t0:t1], bank[:, 0:t1 - t0], ACT.Copy,
                                                 scale=col["L0_xattn_gkv"][:, n:n + 1]).then_inc(turned.sem(0), 1)
                        if kind == "xturn":
                            nc.scalar.activation(hT[:, n, :], bank[:, :], ACT.Copy,
                                                 scale=col["L0_xattn_gq"][:, n:n + 1]).then_inc(turned.sem(0), 1)
                        if kind in ("key", "query"):
                            cw = splits[u][2][1]
                            act.wait_ge(*big_full.done(A, b, k))
                            act.wait_ge(*parts_stored.before(A, b, u))
                            scale = SCALE if kind == "query" else 1.0
                            nc.scalar.activation(proj[:, u % 2, 0:cw], bank[:, 0:cw], ACT.Copy, scale=scale)
                            nc.scalar.activation(parts[:, u % 2, 0, 0:cw], bank[:, 0:cw], ACT.Copy, scale=scale).then_inc(proj_made.sem(u), 1)
                            u += 1

            @block.tensor
            def _(pe):
                pe.wait_ge(constants, 16 * n_const)
                pe.wait_ge(ident_made, 4)

                with pe.Fori(0, B) as b:
                    for k, (kind, n, what) in enumerate(plan):
                        bank = psum[:, k % 8]
                        if k == 0:
                            pe.wait_ge(*v_made.before(A, b, 0))
                            pe.wait_ge(*proj_made.before(A, b, 0))
                            pe.wait_ge(*proj_made.before(A, b, 1))
                        if k >= 8:
                            signal, use = reader[k - 8]
                            pe.wait_ge(*signal.done(A, b, use))
                        if kind == "turn":
                            pe.wait_ge(*hat_made.done(A, b, what[-1]))
                            for i, t in enumerate(what):
                                r = L0.rows[t]
                                last = nc.tensor.transpose(bank[:, i * P:i * P + r], c_tok[0:r, t, n * P:(n + 1) * P], ident[0:r, 0:r])
                        if kind == "xturn":
                            pe.wait_ge(*hat_made.done(A, b, NTT - 1))
                            for t in range(NQT):
                                last = nc.tensor.transpose(bank[:, t * P:(t + 1) * P], x_hat[:, t, n * P:(n + 1) * P], ident[:, :])
                        if kind == "key" and what == (0, L0.chunks[0]):
                            if n == 0:
                                pe.wait_ge(*turned.done(A, b, DC * len(t_groups) - 1))
                            else:
                                pe.wait_ge(*raw_loaded.done(A, b, 0))
                        if kind == "query" and n == 0:
                            pe.wait_ge(*turned.done(A, b, n_turn - 1))
                        if kind == "key":
                            o, (c0, cw) = what
                            for c in range(DC):
                                last = nc.tensor.matmul(bank[:, 0:cw], kv_jobs[n][1][:, c, o * P:(o + 1) * P],
                                                        kv_jobs[n][3][:, c, c0:c0 + cw], start=c == 0, stop=c == DC - 1)
                        if kind == "query":
                            for c in range(DC):
                                last = nc.tensor.matmul(bank[:, :], w["L0_xattn_wq"][:, c, n * P:(n + 1) * P], hT[:, c, :],
                                                        start=c == 0, stop=c == DC - 1)
                        if kind == "value":
                            for i, t in enumerate(what):
                                r = L0.rows[t]
                                for c in range(DC):
                                    last = nc.tensor.matmul(bank[0:r, i * D:(i + 1) * D], kv_jobs[n][3][:, c, t * P:t * P + r],
                                                            kv_jobs[n][2][:, c, :], start=c == 0, stop=c == DC - 1)
                        last.then_inc(big_full.sem(k), 1)

        n_split = {"L0": 4, "self": 2, "cross": 0}
        for st in STAGES:
            for c, uses in ((group_loaded, NG), (max_rows_loaded, NG), (s_full, 2 * NG * st.KT), (masked_done, 2 * NG * st.KT * st.masked),
                            (exp_done, 2 * NG * st.KT), (pv_done, NG * st.KT), (m_full, NG * st.ROWS * st.NCH),
                            (m_free, NG * st.ROWS * st.NCH), (max_step, NG), (max_first, NG), (max_rest, NG), (max_ready, NG),
                            (small_full, len(st.small)), (small_free, len(st.small)), (o_moved, NG), (recip_made, NG),
                            (res_loaded, 1), (res_made, 1), (x_stored, 1), (t_step, 3), (t_rstd, 1), (t_hat, NQT),
                            (h_stored, st is CROSS), (proj_made, n_split[st.name]), (rest_step, n_split[st.name]),
                            (rest_made, n_split[st.name]), (parts_made, n_split[st.name]), (parts_stored, n_split[st.name]),
                            (v_stored, st is L0)):
                c.plan(st.name, int(uses))

        def attention(st):
            N = st.name
            KT, NCH = st.KT, st.NCH
            tail_splits = [x for x in st.small if x[0] in "qk"]
            out_w, out_b = {"L0": (w["L0_xattn_wo"], row["L0_xattn_bo"]), "self": (w["L1_xattn_o_w"], row["L1_xattn_o_b"]),
                            "cross": (w["L1_xattn_co_w"], row["L1_xattn_co_b"])}[N]
            ln_w, ln_b = {"L0": (col["L1_xattn_attn_ln_w"], col["L1_xattn_attn_ln_b"]),
                          "self": (col["L1_xattn_cross_ln_w"], col["L1_xattn_cross_ln_b"]),
                          "cross": (col["L1_xattn_mlp_ln_w"], col["L1_xattn_mlp_ln_b"])}[N]
            q_w = {"L0": w["L1_xattn_q_w"], "self": w["L1_xattn_cq_w"], "cross": None}[N]
            q_b = {"L0": q_bias[:, 0, :], "self": q_bias[:, 1, :], "cross": None}[N]
            k_w, v_w = w["L1_xattn_k_w"], w["L1_xattn_v_w"]
            next_index = min(st.index + 1, len(STAGES) - 1)

            def small_at(count, b, what, last, done):
                use = st.small_use(what, last)
                return count.done(N, b, use) if done else count.before(N, b, use)

            def batches(eng, body):
                with eng.Fori(0, B - 1) as b:
                    body(b, False)
                body(B - 1, True)

            with nc.Block() as block:
                @block.sync
                def _(sp):
                    def load_group(b, k):
                        bb, g = (b, k) if k < NG else (b + 1, k - NG)
                        def heads(dr, part):
                            src = dr[bass.ds(bb, 1), part, g * GW:(g + 1) * GW, :]
                            return src.rearrange("b (h d) t -> (b d) h t", d=DH)
                        loaded = group_loaded.sem(k)
                        for i, (kp, qp) in enumerate(zip(K_PARTS, Q_PARTS)):
                            r0, r1 = i * DH, (i + 1) * DH
                            sp.dma_start(queries[r0:r1, g, :, :], heads(q_dram[st.index], qp)).then_inc(loaded, 16)
                            sp.dma_start(keys[r0:r1, g, :, 0:st.keys], heads(k_dram[st.index], kp)).then_inc(loaded, 16)
                        src = v_dram[st.index][bass.ds(bb, 1), g].rearrange("b p e -> (b p) e")
                        sp.dma_start(values[:, g, 0:KT].rearrange("p t j e -> p (t j e)"), src).then_inc(loaded, 16)

                    def load_max_rows(b, k, use_value):
                        g = k % NG
                        sp.wait_ge(*use_value)
                        for i in range(MR):
                            n = GH * NQT
                            d = queries[PR + i:PR + i + 1, g, :, :]
                            dst = bass.AP(tensor=d.tensor, offset=d.offset, ap=[list(d.ap[0]), [P, n], [1, P]])
                            s = max_rows[i * n:(i + 1) * n, :]
                            sp.dma_start(dst, s).then_inc(max_rows_loaded.sem(k), 16)

                    for k in range(3):
                        load_group(0, k)
                    load_max_rows(0, 0, small_free.done(N, 0, 0))

                    def body(b, last):
                        sp.wait_ge(*t_step.before(N, b, 0))
                        sp.dma_start(x_res[:, :, :], tok(x_dram[st.index], b)).then_inc(res_loaded.sem(0), 16)
                        for g in range(NG):
                            if not (last and g):
                                if g:
                                    sp.wait_ge(*pv_done.done(N, b, g * KT - 1))
                                else:
                                    sp.wait_ge(*pv_done.before(N, b, (NG * KT - 1) % NP))
                                load_group(b, g + 3)
                            if not (last and g == NG - 1):
                                load_max_rows(b, g + 1, small_at(small_free, b, f"max{g}", last, True))
                        sp.wait_ge(*small_at(small_free, b, "out1", last, True))
                        sp.dma_start(tok(x_dram[st.index + 1], b), x_new[:, :, :]).then_inc(x_stored.sem(0), 16)
                        if st is CROSS:
                            sp.wait_ge(*small_at(small_free, b, "hT1", last, True))
                            sp.dma_start(h_dram[bass.ds(b, 1)].rearrange("b p e -> (b p) e"),
                                         hT[:, :, :].rearrange("p c t -> p (c t)")).then_inc(h_stored.sem(0), 16)
                        for u, what in enumerate(tail_splits):
                            o = int(what[1])
                            dr = q_dram[next_index] if what[0] == "q" else k_dram[next_index]
                            sp.wait_ge(*parts_made.done(N, b, u))
                            settle(sp, "sp")
                            dst = dr[bass.ds(b, 1), :, o * P:(o + 1) * P, :].rearrange("b a p t -> p (b a) t")
                            sp.dma_start(dst, parts[:, u % 2, :, :]).then_inc(parts_stored.sem(u), 16)
                        if st is L0:
                            sp.wait_ge(*small_at(small_free, b, "v1", last, True))
                            dst = v_dram[1][bass.ds(b, 1)].rearrange("b g p e -> p (b g) e")
                            sp.dma_start(dst, v_stage[:, :, 0:NQT].rearrange("p g t j e -> p g (t j e)")).then_inc(v_stored.sem(0), 16)

                    batches(sp, body)
                    sp.wait_ge(*x_stored.done(N, B - 1, 0))
                    if st is CROSS:
                        sp.wait_ge(*h_stored.done(N, B - 1, 0))
                    for u in range(len(tail_splits))[-2:]:
                        sp.wait_ge(*parts_stored.done(N, B - 1, u))
                    if st is L0:
                        sp.wait_ge(*v_stored.done(N, B - 1, 0))

                @block.gpsimd
                def _(pool):
                    if st is L0:
                        for g in range(NG):
                            words = keys_flat[PR:PR + MR, g * GH * KV:(g + 1) * GH * KV].bitcast(F32)
                            nc.gpsimd.memset(words, BF16_ONES).then_inc(ones_set, 1)
                        pool.wait_ge(ones_set, NG)

                    def body(b, last):
                        pool.wait_ge(*res_loaded.done(N, b, 0))
                        nc.gpsimd.tensor_tensor(x_res[:, :, :], x_res[:, :, :], out_b.unsqueeze(1).broadcast_to([P, NQT, D]),
                                                ALU.add).then_inc(res_made.sem(0), 1)
                        pool.wait_ge(*t_step.done(N, b, 2))
                        nc.gpsimd.tensor_tensor(rstd[:, 0:NQT], spread[:, 0, 0:NQT], neg_half[:, 0:NQT], ALU.pow).then_inc(t_rstd.sem(0), 1)
                        for u in range(len(tail_splits)):
                            pool.wait_ge(*rest_made.done(N, b, u))
                            nc.gpsimd.tensor_tensor(parts[:, u % 2, 2, :], proj[:, u % 2, :], parts[:, u % 2, 1, :],
                                                    ALU.subtract).then_inc(parts_made.sem(u), 1)

                    with pool.Fori(0, B) as b:
                        body(b, False)

                @block.tensor
                def _(pe):
                    def group_maxima(b, k, some):
                        g = k % NG
                        for r in some:
                            j, qt = divmod(r, NQT)
                            if r == 0:
                                pe.wait_ge(*group_loaded.done(N, b, k))
                            for c, (c0, cw) in enumerate(st.chunks):
                                use = (k * st.ROWS + r) * NCH + c
                                pe.wait_ge(*m_free.before(N, b, use))
                                nc.tensor.matmul(m_ps[:, use % 2, 0:cw], queries[0:PR, g, j, qt * P:(qt + 1) * P],
                                                 keys[0:PR, g, j, c0:c0 + cw], start=True, stop=True).then_inc(m_full.sem(use), 1)

                    def turn_maxima(b, k, before):
                        pe.wait_ge(*before)
                        pe.wait_ge(*max_ready.done(N, b, k))
                        nc.tensor.matmul(small[0:MR * st.ROWS, 0:P], max_parts[:, :], ident_b[:, :],
                                         start=True, stop=True).then_inc(small_full.sem(0), 1)

                    def scores(b, g, t):
                        r = st.rows[t]
                        if t == 0:
                            pe.wait_ge(*max_rows_loaded.done(N, b, g))
                        for u in range(2):
                            use = 2 * (g * KT + t) + u
                            pe.wait_ge(*exp_done.before(N, b, use))
                            for i in range(2):
                                last = nc.tensor.matmul(s_ps[0:r, u, i, :], keys[0:PR + MR, g, 2 * u + i, t * P:t * P + r],
                                                        queries[0:PR + MR, g, 2 * u + i, :], start=True, stop=True)
                            last.then_inc(s_full.sem(use), 1)

                    def weighted_sums(b, i):
                        g, t = divmod(i, KT)
                        r = st.rows[t]
                        for u in range(2):
                            pe.wait_ge(*exp_done.done(N, b, 2 * i + u))
                        if t == 0:
                            pe.wait_ge(*o_moved.before(N, b, g))
                        for j in range(GH):
                            last = nc.tensor.matmul(o_ps[32 * j:32 * j + VH, :], values[0:r, g, t, j, :],
                                                    probs[0:r, i % NP, j * S:(j + 1) * S], start=t == 0, stop=t == KT - 1,
                                                    tile_position=(0, 32 * j), skip_group_check=True)
                        last.then_inc(pv_done.sem(i), 1)

                    def turn_sums(b, g, last):
                        pe.wait_ge(*small_at(small_free, b, f"turn{g}", last, False))
                        pe.wait_ge(*o_moved.done(N, b, g))
                        for t in range(NQT):
                            mm = nc.tensor.transpose(small[:, t * P:(t + 1) * P], o_sum[:, t * P:(t + 1) * P], ident[:, :])
                        mm.then_inc(small_full.sem(0), 1)

                    def tail(b, last):
                        for what in ("oT0", "oT1"):
                            c = int(what[-1])
                            pe.wait_ge(*small_at(small_free, b, what, last, False))
                            for t in range(NQT):
                                mm = nc.tensor.transpose(small[:, t * P:(t + 1) * P], o_tok[:, t, c * P:(c + 1) * P], ident[:, :])
                            mm.then_inc(small_full.sem(0), 1)
                        for what in ("out0", "out1"):
                            pe.wait_ge(*small_at(small_free, b, what, last, False))
                            for i in range(2):
                                t = 2 * int(what[-1]) + i
                                for c in range(DC):
                                    mm = nc.tensor.matmul(small[:, i * D:(i + 1) * D], oT[:, c, t * P:(t + 1) * P], out_w[:, c, :],
                                                          start=c == 0, stop=c == DC - 1)
                            mm.then_inc(small_full.sem(0), 1)
                        for what in ("hT0", "hT1"):
                            c = int(what[-1])
                            pe.wait_ge(*small_at(small_free, b, what, last, False))
                            for t in range(NQT):
                                pe.wait_ge(*t_hat.done(N, b, t))
                                mm = nc.tensor.transpose(small[:, t * P:(t + 1) * P], x_hat[:, t, c * P:(c + 1) * P], ident[:, :])
                            mm.then_inc(small_full.sem(0), 1)
                        for what in tail_splits:
                            o = int(what[-1])
                            wt = q_w if what[0] == "q" else k_w
                            pe.wait_ge(*small_at(small_free, b, what, last, False))
                            for c in range(DC):
                                mm = nc.tensor.matmul(small[:, :], wt[:, c, o * P:(o + 1) * P], hT[:, c, :],
                                                      start=c == 0, stop=c == DC - 1)
                            mm.then_inc(small_full.sem(0), 1)
                        if st is L0:
                            for what in ("v0", "v1"):
                                pe.wait_ge(*small_at(small_free, b, what, last, False))
                                for i in range(2):
                                    t = 2 * int(what[-1]) + i
                                    for c in range(DC):
                                        mm = nc.tensor.matmul(small[:, i * D:(i + 1) * D], hT[:, c, t * P:(t + 1) * P], v_w[:, c, :],
                                                              start=c == 0, stop=c == DC - 1)
                                mm.then_inc(small_full.sem(0), 1)

                    group_maxima(0, 0, range(st.ROWS))
                    turn_maxima(0, 0, small_free.before(N, 0, 0))
                    if st is L0:
                        pe.wait_ge(ones_set, NG)

                    def body(b, last):
                        for i in range(NG * KT):
                            g, t = divmod(i, KT)
                            scores(b, g, t)
                            more = not (last and g == NG - 1)
                            if more:
                                group_maxima(b, g + 1, st.share[t])
                            if i:
                                weighted_sums(b, i - 1)
                            if g and t == 1:
                                turn_sums(b, g - 1, last)
                            if more and t == KT - 1:
                                turn_maxima(b, g + 1, small_at(small_free, b, f"max{g}", last, False))
                        weighted_sums(b, NG * KT - 1)
                        turn_sums(b, NG - 1, last)
                        tail(b, last)

                    batches(pe, body)

                @block.scalar
                def _(act):
                    def exps(b, i):
                        g, t = divmod(i, KT)
                        r = st.rows[t]
                        if i >= 0:
                            act.wait_ge(*pv_done.before(N, b, i))
                        for u in range(2):
                            use = 2 * i + u
                            act.wait_ge(*(masked_done if st.masked else s_full).done(N, b, use))
                            nc.scalar.activation(probs[0:r, i % NP, 2 * u * S:2 * (u + 1) * S], s_ps[0:r, u].rearrange("p j t -> p (j t)"),
                                                 ACT.Exp).then_inc(exp_done.sem(use), 1)

                    def move_sums(b, g, last):
                        act.wait_ge(*pv_done.done(N, b, (g + 1) * KT - 1))
                        act.wait_ge(*small_at(small_full, b, f"turn{g}", last, False))
                        nc.scalar.activation(o_sum[:, :], o_ps[:, :], ACT.Copy).then_inc(o_moved.sem(0), 1)

                    def tail(b, last):
                        for what in ("oT0", "oT1"):
                            act.wait_ge(*small_at(small_full, b, what, last, True))
                            nc.scalar.activation(oT[:, int(what[-1]), :], small[:, :], ACT.Copy).then_inc(small_free.sem(0), 1)
                        for what in ("hT0", "hT1"):
                            c = int(what[-1])
                            act.wait_ge(*small_at(small_full, b, what, last, True))
                            if st is CROSS and c == 0:
                                act.wait_ge(*h_stored.before(N, b, 0))
                            nc.scalar.activation(hT[:, c, :], small[:, :], ACT.Identity, bias=ln_b[:, c:c + 1],
                                                 scale=ln_w[:, c:c + 1]).then_inc(small_free.sem(0), 1)
                        for u, what in enumerate(tail_splits):
                            o = int(what[-1])
                            act.wait_ge(*small_at(small_full, b, what, last, True))
                            act.wait_ge(*parts_stored.before(N, b, u))
                            for dst in (proj[:, u % 2, :], parts[:, u % 2, 0, :]):
                                if what[0] == "q":
                                    mv = nc.scalar.activation(dst, small[:, :], ACT.Identity, bias=q_b[:, o:o + 1], scale=SCALE)
                                else:
                                    mv = nc.scalar.activation(dst, small[:, :], ACT.Copy)
                            mv.then_inc(small_free.sem(0), 1)

                    def body(b, last):
                        for i in range(NG * KT):
                            g, t = divmod(i, KT)
                            exps(b, i)
                            if g and t == 0:
                                move_sums(b, g - 1, last)
                        move_sums(b, NG - 1, last)
                        tail(b, last)

                    batches(act, body)

                @block.vector
                def _(dve):
                    def group_maxima(b, k, some):
                        for r in some:
                            for c, (c0, cw) in enumerate(st.chunks):
                                use = (k * st.ROWS + r) * NCH + c
                                dve.wait_ge(*m_full.done(N, b, use))
                                if st.masked:
                                    settle(dve, "dve")
                                dst = part_max[:, r * NCH + c:r * NCH + c + 1]
                                if st.masked:
                                    op = nc.vector.tensor_tensor_reduce(junk[:, use % 2, 0:cw], m_ps[:, use % 2, 0:cw],
                                                                        mask_q[:, r % NQT, c0:c0 + cw], 1.0, LOWEST, ALU.add, ALU.max, dst)
                                else:
                                    op = nc.vector.tensor_reduce(dst, m_ps[:, use % 2, 0:cw], AX.X, ALU.max)
                                op.then_inc(m_free.sem(use), 1)

                    def split_maxima(b, k):
                        last_use = (k + 1) * st.ROWS * NCH - 1
                        for use in (last_use - 1, last_use):
                            dve.wait_ge(*m_free.done(N, b, use))
                        n = st.ROWS
                        nc.vector.tensor_reduce(neg_max[:, :], part_max[:, 0:n * NCH].rearrange("p (r c) -> p r c", c=NCH),
                                                AX.X, ALU.max, negate=True).then_inc(max_step.sem(0), 1)
                        dve.wait_ge(*max_step.done(N, b, k))
                        nc.vector.tensor_copy(max_parts[:, 0:n], neg_max[:, :]).then_inc(max_first.sem(0), 1)
                        dve.wait_ge(*max_first.done(N, b, k))
                        nc.vector.tensor_tensor(max_parts[:, n:2 * n], neg_max[:, :], max_parts[:, 0:n], ALU.subtract).then_inc(max_ready.sem(0), 1)

                    def move_maxima(full):
                        dve.wait_ge(*full)
                        nc.vector.tensor_copy(max_rows[:, :], small[0:MR * st.ROWS, 0:P]).then_inc(small_free.sem(0), 1)

                    def add_mask(b, i):
                        t = i % KT
                        for u in range(2):
                            use = 2 * i + u
                            dve.wait_ge(*s_full.done(N, b, use))
                            nc.vector.tensor_tensor(s_ps[:, u], s_ps[:, u], mask_k[:, t, :].unsqueeze(1).broadcast_to([P, 2, S]),
                                                    ALU.add).then_inc(masked_done.sem(use), 1)

                    def normalize(b, g, last):
                        dve.wait_ge(*small_at(small_full, b, f"turn{g}", last, True))
                        v = small[:, :].rearrange("p (t j r) -> p t j r", t=NQT, j=GH)
                        nc.vector.reciprocal(recip[:, :, :], v[:, :, :, DH]).then_inc(recip_made.sem(0), 1)
                        dve.wait_ge(*recip_made.done(N, b, g))
                        dst = o_tok[:, :, g * GW:(g + 1) * GW].rearrange("p t (j d) -> p t j d", j=GH)
                        nc.vector.tensor_tensor(dst, v[:, :, :, 0:DH], recip[:, :, :].unsqueeze(3).broadcast_to([P, NQT, GH, DH]),
                                                ALU.mult).then_inc(small_free.sem(0), 1)

                    def tail(b, last):
                        dve.wait_ge(*res_made.done(N, b, 0))
                        dve.wait_ge(*x_stored.before(N, b, 0))
                        for what in ("out0", "out1"):
                            t = 2 * int(what[-1])
                            dve.wait_ge(*small_at(small_full, b, what, last, True))
                            nc.vector.tensor_tensor(x_new[:, t:t + 2, :], small[:, :].rearrange("p (t d) -> p t d", t=2), x_res[:, t:t + 2, :],
                                                    ALU.add).then_inc(small_free.sem(0), 1)
                        dve.wait_ge(*small_at(small_free, b, "out1", last, True))
                        for t in range(NQT):
                            op = nc.vector.bn_stats(stats[:, t, :], x_new[:, t, :])
                        op.then_inc(t_step.sem(0), 1)
                        dve.wait_ge(*t_step.done(N, b, 0))
                        settle(dve, "dve")
                        for t in range(NQT):
                            op = nc.vector.bn_aggr(mean_var[:, t, :], stats[:, t, :])
                        op.then_inc(t_step.sem(0), 1)
                        dve.wait_ge(*t_step.done(N, b, 1))
                        nc.vector.tensor_scalar(spread[:, 0, 0:NQT], mean_var[:, 0:NQT, 1], EPS_LN, None, ALU.add).then_inc(t_step.sem(0), 1)
                        dve.wait_ge(*t_rstd.done(N, b, 0))
                        for t in range(NQT):
                            nc.vector.tensor_scalar(x_hat[:, t, :], x_new[:, t, :], mean_var[:, t, 0:1], rstd[:, t:t + 1],
                                                    ALU.subtract, ALU.mult).then_inc(t_hat.sem(0), 1)
                        for u, what in enumerate(tail_splits):
                            f, p = proj[:, u % 2, :], parts[:, u % 2]
                            dve.wait_ge(*small_at(small_free, b, what, last, True))
                            nc.vector.tensor_tensor(f, f, p[:, 0, :], ALU.subtract).then_inc(rest_step.sem(u), 1)
                            dve.wait_ge(*rest_step.done(N, b, u))
                            nc.vector.tensor_copy(p[:, 1, :], f).then_inc(rest_made.sem(u), 1)
                        if st is L0:
                            dve.wait_ge(*v_stored.before(N, b, 0))
                            for what in ("v0", "v1"):
                                t = 2 * int(what[-1])
                                dve.wait_ge(*small_at(small_full, b, what, last, True))
                                for i in range(2):
                                    op = nc.vector.tensor_tensor(staged(t + i), by_head(small[:, i * D:(i + 1) * D]),
                                                                 by_head(row["L1_xattn_v_b"]), ALU.add)
                                op.then_inc(small_free.sem(0), 1)

                    group_maxima(0, 0, range(st.ROWS))
                    split_maxima(0, 0)
                    move_maxima(small_full.done(N, 0, 0))

                    def body(b, last):
                        for i in range(NG * KT):
                            g, t = divmod(i, KT)
                            more = not (last and g == NG - 1)
                            if st.masked:
                                add_mask(b, i)
                            if more:
                                group_maxima(b, g + 1, st.share[t])
                            if g and t == 1:
                                normalize(b, g - 1, last)
                            if more and t == KT - 1:
                                split_maxima(b, g + 1)
                                move_maxima(small_at(small_full, b, f"max{g}", last, True))
                        normalize(b, NG - 1, last)
                        tail(b, last)

                    batches(dve, body)

        for st in STAGES:
            attention(st)

        M = "mlp"
        N_F = FC + NQT // 2
        for c, uses in ((h_loaded, 1), (res_loaded, 1), (res_made, 1), (x_stored, 1), (f_full, N_F), (gelu_done, FC),
                        (y_made, NQT // 2)):
            c.plan(M, uses)

        with nc.Block() as block:
            @block.sync
            def _(sp):
                sp.dma_start(fc1, a["L1_xattn_fc1_w"].rearrange("(c p) f -> p c f", p=P)).then_inc(fc_loaded, 16)
                sp.dma_start(fc2, a["L1_xattn_fc2_w"].rearrange("(c p) d -> p c d", p=P)).then_inc(fc_loaded, 16)

                def load_h(b):
                    sp.dma_start(hT[:, :, :].rearrange("p c t -> p (c t)"),
                                 h_dram[bass.ds(b, 1)].rearrange("b p e -> (b p) e")).then_inc(h_loaded.sem(0), 16)

                def load_x(b):
                    sp.dma_start(x_res[:, :, :], tok(x_dram[3], b)).then_inc(res_loaded.sem(0), 16)

                load_h(0)
                load_x(0)

                def body(b, last):
                    if not last:
                        sp.wait_ge(*f_full.done(M, b, FC - 1))
                        load_h(b + 1)
                    sp.wait_ge(*y_made.done(M, b, NQT // 2 - 1))
                    sp.dma_start(tok(out, b), x_new[:, :, :]).then_inc(x_stored.sem(0), 16)
                    if not last:
                        load_x(b + 1)

                with sp.Fori(0, B - 1) as b:
                    body(b, False)
                body(B - 1, True)
                sp.wait_ge(*x_stored.done(M, B - 1, 0))

            @block.gpsimd
            def _(pool):
                with pool.Fori(0, B) as b:
                    pool.wait_ge(*res_loaded.done(M, b, 0))
                    nc.gpsimd.tensor_tensor(x_res[:, :, :], x_res[:, :, :], row["L1_xattn_fc2_b"].unsqueeze(1).broadcast_to([P, NQT, D]),
                                            ALU.add).then_inc(res_made.sem(0), 1)

            @block.tensor
            def _(pe):
                pe.wait_ge(fc_loaded, 32)
                with pe.Fori(0, B) as b:
                    pe.wait_ge(*h_loaded.done(M, b, 0))
                    for m in range(FC):
                        pe.wait_ge(*gelu_done.before(M, b, 0))
                        if m < NQT // 2:
                            pe.wait_ge(*y_made.before(M, b, 0))
                        for c in range(DC):
                            last = nc.tensor.matmul(psum[:, m], fc1[:, c, m * P:(m + 1) * P], hT[:, c, :], start=c == 0, stop=c == DC - 1)
                        last.then_inc(f_full.sem(m), 1)
                    for y in range(NQT // 2):
                        pe.wait_ge(*gelu_done.done(M, b, FC - 1))
                        for i in range(2):
                            t = 2 * y + i
                            for m in range(FC):
                                last = nc.tensor.matmul(psum[:, y, i * D:(i + 1) * D], h1[:, 0, m, t * P:(t + 1) * P], fc2[:, m, :],
                                                        start=m == 0, stop=m == FC - 1)
                        last.then_inc(f_full.sem(FC + y), 1)

            @block.scalar
            def _(act):
                with act.Fori(0, B) as b:
                    for m in range(FC):
                        act.wait_ge(*f_full.done(M, b, m))
                        nc.scalar.activation(h1[:, 0, m, :], psum[:, m], ACT.Gelu, bias=fc1_b[:, m:m + 1]).then_inc(gelu_done.sem(0), 1)

            @block.vector
            def _(dve):
                with dve.Fori(0, B) as b:
                    dve.wait_ge(*res_made.done(M, b, 0))
                    dve.wait_ge(*x_stored.before(M, b, 0))
                    for y in range(NQT // 2):
                        dve.wait_ge(*f_full.done(M, b, FC + y))
                        nc.vector.tensor_tensor(x_new[:, 2 * y:2 * y + 2, :], psum[:, y].rearrange("p (t d) -> p t d", t=2),
                                                x_res[:, 2 * y:2 * y + 2, :], ALU.add).then_inc(y_made.sem(0), 1)


_TURNED = [n for n in (
    "L0_xattn_wq", "L0_xattn_wk", "L0_xattn_wv", "L0_xattn_wo", "L1_xattn_q_w", "L1_xattn_k_w", "L1_xattn_v_w",
    "L1_xattn_o_w", "L1_xattn_cq_w", "L1_xattn_ck_w", "L1_xattn_cv_w", "L1_xattn_co_w", "L1_xattn_fc1_w", "L1_xattn_fc2_w")]


def kernel(**inputs):
    import numpy as np
    import concourse.bacc as bacc
    from concourse.bass_utils import run_bass_kernel_spmd

    laid = {}
    for name, value in inputs.items():
        value = np.asarray(value)
        if name in _TURNED:
            laid[name] = np.ascontiguousarray(value.T)
        elif name == "ctx_1024":
            laid["ctx"] = np.ascontiguousarray(value)
            laid["ctx_T"] = np.ascontiguousarray(value.transpose(0, 2, 1))
        elif name == "mask_SxS_fc0":
            laid["mask"] = np.ascontiguousarray(value)
            laid["mask_T"] = np.ascontiguousarray(value.T)
        elif name in ROW_NAMES or name == "x":
            laid[name] = np.ascontiguousarray(value)
        if name in COL_NAMES:
            laid[f"{name}_col"] = np.ascontiguousarray(value.reshape(-1, P).T)
    nc = bacc.Bacc("TRN2", target_bir_lowering=False, num_devices=1)
    arrays, a = {}, {}
    for name, value in laid.items():
        arrays[f"in_{name}"] = value
        a[name] = nc.dram_tensor(f"in_{name}", value.shape, mybir.dt.from_np(value.dtype), kind="ExternalInput").ap()
    out = nc.dram_tensor("out_x", (B, S, D), F32, kind="ExternalOutput").ap()
    build(nc, a, out)
    r = run_bass_kernel_spmd(nc, [arrays], core_ids=[0])
    return r.results[0]["out_x"]
```

```python
from contextlib import ExitStack

import concourse.bass as bass
import concourse.mybir as mybir

P = 128
B, S, D = 8, 512, 256
H, DH = 16, 16
KV = 1601
F = 1024
GH = 4
NG = H // GH
GW = GH * DH
VH = DH + 1
DC = D // P
FC = F // P
NQT = S // P
KVT = -(-KV // P)
SCALE = DH ** -0.5
EPS_RMS, EPS_LN = 1e-6, 1e-5
K_PARTS = [0, 0, 0, 1, 1, 2]
Q_PARTS = [0, 1, 2, 0, 1, 0]
PR = DH * len(K_PARTS)
MR = 3
MAX_ROWS = GH * (S // P)
SB = 3
MB = 3
NP = 2
DVE_MASKED = (0, 2)
ORDER = [("scores", 0), ("maxima", 0), ("scores", 1), ("scores", 2), ("maxima", 1), ("scores", 3), ("maxima", 2),
         ("sums", 0), ("maxima", 3)]
N_MAX = sum(what == "maxima" for what, _ in ORDER)
READ_AFTER, REST_AFTER = 0, 2
LOAD_PIECES = 4
NCP = 4
FLAT = GH * NG * KV

ROW_NAMES = ["L0_xattn_gq", "L0_xattn_bo", "L1_xattn_v_b", "L1_xattn_o_b",
             "L1_xattn_cv_b", "L1_xattn_co_b", "L1_xattn_fc2_b"]
COL_NAMES = ["L0_xattn_gq", "L0_xattn_gkv", "L1_xattn_attn_ln_w", "L1_xattn_attn_ln_b",
             "L1_xattn_cross_ln_w", "L1_xattn_cross_ln_b", "L1_xattn_mlp_ln_w", "L1_xattn_mlp_ln_b",
             "L1_xattn_q_b", "L1_xattn_cq_b", "L1_xattn_fc1_b"]

LOWEST = -3.4028234e38
MASK_FLOOR = -3.0e38
BF16_ONES = 1.0019379

F32 = mybir.dt.float32
BF16 = mybir.dt.bfloat16
ALU = mybir.AluOpType
ACT = mybir.ActivationFunctionType
AX = mybir.AxisListType


class Count:

    def __init__(self, sems, unit=1, start=1):
        self.sems, self.unit = sems, unit
        self.base, self.per = {}, {}
        self.total = [start] * len(sems)

    def plan(self, stage, uses, times=B):
        n = len(self.sems)
        self.base[stage] = list(self.total)
        self.per[stage] = [len(range(s, uses, n)) for s in range(n)]
        self.total = [t + times * p for t, p in zip(self.total, self.per[stage])]

    def sem(self, k):
        return self.sems[k % len(self.sems)]

    def before(self, stage, b, k):
        s = k % len(self.sems)
        fixed = (self.base[stage][s] + k // len(self.sems)) * self.unit
        return self.sems[s], b * (self.per[stage][s] * self.unit) + fixed

    def done(self, stage, b, k):
        sem, value = self.before(stage, b, k)
        return sem, value + self.unit


class Stage:

    def __init__(self, name, index, keys, masked):
        self.name, self.index, self.keys, self.masked = name, index, keys, masked
        self.KT = -(-keys // P)
        self.steps = NG * self.KT
        self.NCH = -(-keys // 512)
        width = -(-keys // self.NCH)
        self.chunks = [(c * width, min(width, keys - c * width)) for c in range(self.NCH)]
        self.rows = [min(P, keys - t * P) for t in range(self.KT)]
        self.max_uses = MAX_ROWS * self.NCH
        self.lead = 4 if self.KT > 4 else 3
        self.turn_at = 1 if self.KT > 4 else 3
        self.tail = ["turn3", "oT0", "oT1", "out0", "out1", "hT0", "hT1"]
        self.tail += {"L0": ["q0", "q1", "k0", "k1", "v0", "v1"], "self": ["q0", "q1"], "cross": []}[name]


L0, SELF, CROSS = Stage("L0", 0, KV, False), Stage("self", 1, S, True), Stage("cross", 2, KV, False)
STAGES = (L0, SELF, CROSS)


def cut(some, n):
    return some[-(-len(some) * n // N_MAX):-(-len(some) * (n + 1) // N_MAX)]


class Body:

    def __init__(self, st, kind, r=0):
        self.st, self.kind, self.r = st, kind, r
        self.b = {"first": 0, "mid": r + 1, "last": B - 1, "end": B}[kind]
        self.name = f"{st.name} {kind}"
        if kind == "first":
            self.tail_st, self.tail_b = (STAGES[st.index - 1], B - 1) if st.index else (None, None)
        else:
            self.tail_st = st
            self.tail_b = {"mid": r, "last": B - 2, "end": B - 1}[kind]
        self.small = [[] for _ in range(st.steps)]
        if kind != "end":
            for g in range(NG):
                if g:
                    self.small[g * st.KT + st.turn_at].append(("turn", g - 1))
                if self.following(g + 1):
                    self.small[(g + 1) * st.KT - st.lead].append(("max", g + 1))
        if self.tail_st is not None:
            items = self.tail_st.tail
            if kind == "end":
                at = [0] * len(items)
            elif st.KT > 4:
                at = [n for n in range(1, st.steps) if n % 3 == 1 and not self.small[n]]
            else:
                at = [2, 3, 3, 4, 6, 8, 10, 12, 14] if len(items) < 10 else [2, 3, 3, 4, 6, 8, 10, 10, 12, 12, 14, 14, 15]
            for n, item in zip(at, items):
                self.small[n].append(("tail", item))
        self.order = [x for step in self.small for x in step]

    def following(self, k):
        if k < NG:
            return self.st, self.b, k
        if self.kind != "last":
            return self.st, self.b + 1, k - NG
        if self.st.index + 1 < len(STAGES):
            return STAGES[self.st.index + 1], 0, k - NG
        return None

    def share(self, i):
        if self.kind == "end":
            return None, []
        ahead = self.st.lead
        g, t = divmod(i + ahead, self.st.KT)
        to = self.following(g + 1)
        if not to or (self.kind == "last" and g == NG):
            return None, []
        slots = self.st.KT
        if self.kind == "first" and g == 0:
            t, slots = t - ahead, slots - ahead
        n = to[0].max_uses
        return to, [c for c in range(n) if c * slots // n == t]

    def step_of(self, item):
        for i, step in enumerate(self.small):
            if item in step:
                return i
        return None


def build(nc, a, out):
    ctx = ExitStack()
    with ctx:
        def sb(name, shape, dt=F32):
            return ctx.enter_context(nc.sbuf_tensor(name, shape, dt))

        counts = []

        def sems(name, n=1, unit=1):
            counts.append(Count([ctx.enter_context(nc.semaphore(f"{name}{i}" if n > 1 else name)) for i in range(n)], unit))
            return counts[-1]

        def sem(name):
            return ctx.enter_context(nc.semaphore(name))

        def dram(name, shape, dt=F32):
            return nc.dram_tensor(name, shape, dt).ap()

        k_dram = [dram(f"k_parts_{s.name}", (B, 3, D, s.keys), BF16) for s in STAGES]
        q_dram = [dram(f"q_parts_{s.name}", (B, 3, D, S), BF16) for s in STAGES]
        v_dram = [dram(f"v_{s.name}", (B, NG, P, s.KT * GH * VH)) for s in STAGES]
        x_dram = [dram(f"x_{i}", (B, S, D)) for i in range(4)]
        h_dram = dram("h_mlp", (B, P, DC * S))

        keys_flat = sb("keys_flat", [P, FLAT], BF16)
        keys = keys_flat[:, :].rearrange("p (g j t) -> p g j t", g=NG, j=GH)
        queries = sb("queries", [P, NG, GH, S], BF16)
        values = sb("values", [P, NG, KVT, GH, VH])
        probs = sb("probs", [P, NP, GH * S])
        v_stage = sb("v_stage", [P, NG, KVT, GH, VH])
        w_names = ["L0_xattn_wq", "L0_xattn_wk", "L0_xattn_wv", "L0_xattn_wo",
                   "L1_xattn_q_w", "L1_xattn_k_w", "L1_xattn_v_w", "L1_xattn_o_w",
                   "L1_xattn_cq_w", "L1_xattn_ck_w", "L1_xattn_cv_w", "L1_xattn_co_w"]
        weights = sb("weights", [P, len(w_names), DC, D])
        w = {n: weights[:, i] for i, n in enumerate(w_names)}
        mask_q = sb("mask_q", [P, NQT, S])
        mask_k = sb("mask_k", [P, S // P, S])
        mask_parts = sb("mask_parts", [P, 3, S // P, S], BF16)
        x_res = sb("x_res", [P, NQT, D])
        x_new = sb("x_new", [P, NQT, D])
        x_hat = sb("x_hat", [P, NQT, D])
        hT = sb("hT", [P, DC, S])
        o_tok = sb("o_tok", [P, NQT, D])
        oT = sb("oT", [P, DC, S])
        o_sum = sb("o_sum", [P, S])
        proj = sb("proj", [P, 2, S])
        parts = sb("parts", [P, 2, 3, S], BF16)
        rows = sb("rows", [P, len(ROW_NAMES), D])
        row = {n: rows[:, i] for i, n in enumerate(ROW_NAMES)}
        cols = sb("cols", [P, len(COL_NAMES), DC])
        col = {n: cols[:, i] for i, n in enumerate(COL_NAMES[:-1])}
        fc1_b = sb("fc1_b", [P, FC])
        q_bias = sb("q_bias", [P, 2, DC])
        ident = sb("ident", [P, P])
        ident_b = sb("ident_b", [P, P], BF16)
        neg_half = sb("neg_half", [P, KVT + NQT])
        NTT = KVT + NQT
        stats = sb("stats", [P, NTT, 6])
        mean_var = sb("mean_var", [P, NTT, 2])
        spread = sb("spread", [P, 2, NTT])
        rstd = sb("rstd", [P, NTT])
        part_max = sb("part_max", [P, GH * NQT * 4])
        neg_max = sb("neg_max", [P, GH * NQT])
        max_parts = sb("max_parts", [P, MR * GH * NQT], BF16)
        max_rows = sb("max_rows", [MR * GH * NQT, P], BF16)
        recip = sb("recip", [P, NQT, GH])

        f32_flat = keys_flat[:, :].bitcast(F32)
        c_tok = f32_flat[:, 0:KVT * D].rearrange("p (t d) -> p t d", t=KVT)
        at = KVT * D
        c_raw = f32_flat[:, at:at + DC * KV].rearrange("p (c t) -> p c t", c=DC)
        at += DC * KV
        c_norm = f32_flat[:, at:at + DC * KV].rearrange("p (c t) -> p c t", c=DC)
        c_proj = probs[:, 0].rearrange("p (i t) -> p i t", i=NCP)
        c_parts = queries[:, 0:3].rearrange("p a g t -> p (a g t)").rearrange("p (i k t) -> p i k t", i=NCP, k=3)
        junk = [v_stage[:, i, NQT:KVT].rearrange("p t j e -> p (t j e)")[:, 0:S // 2].bitcast(BF16) for i in range(MB)]
        fc1 = mask_q[:, :, :].rearrange("p t k -> p (t k)").rearrange("p (c f) -> p c f", c=DC)
        fc2 = mask_k[:, :, :].rearrange("p t q -> p (t q)").rearrange("p (c d) -> p c d", c=FC)
        h1 = f32_flat[:, 0:FC * S].rearrange("p (c t) -> p c t", c=FC)

        psum = ctx.enter_context(nc.psum_tensor("psum", [P, 8, 512], F32))
        s_ps = psum[:, 0:SB]
        m_ps = psum[:, SB:SB + MB]
        o_ps = psum[:, 6]
        small = psum[:, 7]

        def tok(dr, b):
            return dr[bass.ds(b, 1)].rearrange("b (t p) d -> p (b t) d", p=P)

        def staged(t, r=P):
            return v_stage[0:r, :, t, :, 0:DH]

        def by_head(ap):
            return ap.rearrange("p (g j d) -> p g j d", g=NG, j=GH)

        constants = sem("constants_loaded")
        late_constants = sem("late_constants_loaded")
        ctx_loaded = sems("ctx_tokens_loaded", unit=16)
        raw_loaded = sems("ctx_raw_loaded", unit=16)
        xin_loaded = sems("x_loaded", unit=16)
        ident_made = sem("ident_made")
        mask_step = sem("mask_split_step")
        bias_made = sem("bias_made")
        consts_set = sem("consts_set")
        norm_step = sems("norm_step")
        rstd_made = sems("rstd_made")
        hat_made = sems("hat_made")
        big_full = sems("bank_full", 8)
        turned = sems("turned")
        proj_made = sems("proj_made", 2)
        rest_step = sems("rest_step", 2)
        rest_made = sems("rest_made", 2)
        parts_made = sems("parts_made", 2)
        parts_stored = sems("parts_stored", 2, 16)
        v_made = sems("v_made")
        v_stored = sems("v_stored", unit=16)
        xn_made = sems("xn_made")
        xn_stored = sems("xn_stored", unit=16)

        c_proj_made = sems("ctx_proj_made", NCP)
        c_rest_step = sems("ctx_rest_step", NCP)
        c_rest_made = sems("ctx_rest_made", NCP)
        c_parts_made = sems("ctx_parts_made", NCP)
        c_parts_stored = sems("ctx_parts_stored", NCP, 16)

        N_LOADS = len(K_PARTS) + len(Q_PARTS) + 1
        group_loaded = sems("group_loaded", NG, 16 * N_LOADS)
        max_rows_loaded = sems("max_rows_loaded", NG, 16 * MR)
        ones_set = sem("ones_set")
        s_full = sems("scores_ready", SB)
        masked_done = sems("masked", SB)
        exp_done = sems("exp_done", SB)
        pv_done = sems("weighted_sum_added", NP)
        m_full = sems("max_scores_ready", MB)
        m_free = sems("max_taken", MB)
        max_step = sems("max_negated")
        max_first = sems("max_first_part")
        max_rest = sems("max_rest")
        max_second = sems("max_second_part")
        max_ready = sems("max_parts_ready")
        small_full = sems("small_bank_full")
        small_free = sems("small_bank_read")
        o_moved = sems("sums_in_sbuf")
        recip_made = sems("reciprocal_made")
        res_loaded = sems("residual_loaded", unit=16)
        res_made = sems("residual_made")
        x_stored = sems("x_stored", unit=16)
        t_step = sems("tail_norm_step")
        t_rstd = sems("tail_rstd_made")
        t_hat = sems("tail_hat_made")
        h_stored = sems("h_stored", unit=16)

        fc_loaded = sem("fc_weights_loaded")
        h_loaded = sems("h_loaded", unit=16)
        f_full = sems("fc_bank_full", 8)
        gelu_done = sems("gelu_done")
        y_made = sems("y_made")
        waited = {"dve": sem("vector_waited"), "sp": sem("sync_waited")}

        with nc.Block() as block:
            @block.sync
            def _(sp):
                for c in counts:
                    for one in c.sems:
                        sp.sem_inc(one, c.unit)

        def settle(eng, name):
            eng.sem_inc(waited[name], 1)

        kv_jobs = [(L0, w["L0_xattn_wk"], w["L0_xattn_wv"], c_norm, None),
                   (CROSS, w["L1_xattn_ck_w"], w["L1_xattn_cv_w"], c_raw, row["L1_xattn_cv_b"])]
        t_groups = [list(range(i, min(i + 4, KVT))) for i in range(0, KVT, 4)]
        v_pairs = [list(range(i, min(i + 2, KVT))) for i in range(0, KVT, 2)]
        plan = [("turn", c, ts) for c in range(DC) for ts in t_groups]
        plan += [("xturn", c, None) for c in range(DC)]
        splits = []
        for n in range(2):
            for o in range(DC):
                for ch in L0.chunks:
                    splits.append((n, o, ch))
                    plan.append(("key", n, (o, ch)))
            plan += [("value", n, ts) for ts in v_pairs]
            if n == 0:
                for o in range(DC):
                    splits.append(("q", o, (0, S)))
                    plan.append(("query", o, None))
        n_turn = sum(p[0] in ("turn", "xturn") for p in plan)
        n_v = len(v_pairs)
        norm_use = len(splits) // 2 - DC
        for c, uses in ((ctx_loaded, LOAD_PIECES + 1), (raw_loaded, LOAD_PIECES), (xin_loaded, 1), (norm_step, 4), (rstd_made, 1),
                        (hat_made, NTT), (big_full, len(plan)), (turned, n_turn),
                        (c_proj_made, len(splits)), (c_rest_step, len(splits)), (c_rest_made, len(splits)), (c_parts_made, len(splits)),
                        (c_parts_stored, len(splits)), (v_made, 2 * n_v), (v_stored, 2), (xn_made, 1), (xn_stored, 1)):
            c.plan("context", uses)
        A = "context"
        early = [("w", n) for n in ("L0_xattn_wk", "L0_xattn_wv", "L0_xattn_wq", "L1_xattn_ck_w", "L1_xattn_cv_w")]
        early += [("row", n) for n in ("L0_xattn_gq", "L1_xattn_cv_b")] + [("col", n) for n in ("L0_xattn_gkv", "L0_xattn_gq")]
        every = [("w", n) for n in w_names] + [("row", n) for n in ROW_NAMES] + [("col", n) for n in COL_NAMES[:-1]]
        late = [x for x in every if x not in early]
        n_const, n_late = len(early), len(late) + 3
        reader, u, v, t = [], 0, 0, 0
        for kind, _, _ in plan:
            if kind in ("turn", "xturn"):
                reader.append((turned, t))
                t += 1
            elif kind == "value":
                reader.append((v_made, v))
                v += 1
            else:
                reader.append((c_proj_made, u))
                u += 1

        with nc.Block() as block:
            @block.sync
            def _(sp):
                full = KVT - 1

                def load_tokens(b, i):
                    t0, t1 = full * i // LOAD_PIECES, full * (i + 1) // LOAD_PIECES
                    src = a["ctx"][bass.ds(b, 1), t0 * P:t1 * P, :].rearrange("b (t p) d -> p (b t) d", p=P)
                    sp.dma_start(c_tok[:, t0:t1, :], src).then_inc(ctx_loaded.sem(0), 16)
                    if i == LOAD_PIECES - 1:
                        rest = a["ctx"][bass.ds(b, 1), full * P:KV, :].rearrange("b p d -> p (b d)")
                        sp.dma_start(c_tok[0:KV - full * P, full, :], rest).then_inc(ctx_loaded.sem(0), 16)
                        sp.dma_start(x_res[:, :, :], tok(a["x"], b)).then_inc(xin_loaded.sem(0), 16)

                def load_raw(b, i):
                    t0, t1 = KV * i // LOAD_PIECES, KV * (i + 1) // LOAD_PIECES
                    src = a["ctx_T"][bass.ds(b, 1), :, t0:t1].rearrange("b (c p) t -> p (b c) t", p=P)
                    sp.dma_start(c_raw[:, :, t0:t1], src).then_inc(raw_loaded.sem(0), 16)

                for i in range(LOAD_PIECES):
                    load_tokens(0, i)
                def load_constant(kind, n, loaded):
                    if kind == "w":
                        sp.dma_start(w[n], a[n].rearrange("(c p) o -> p c o", p=P)).then_inc(loaded, 16)
                    if kind == "row":
                        sp.dma_start(row[n], a[n].rearrange("(a d) -> a d", a=1).broadcast_to([P, D])).then_inc(loaded, 16)
                    if kind == "col":
                        sp.dma_start(col[n], a[n + "_col"]).then_inc(loaded, 16)

                for kind, n in early:
                    load_constant(kind, n, constants)
                for kind, n in late:
                    load_constant(kind, n, late_constants)
                sp.dma_start(fc1_b[:, :], a["L1_xattn_fc1_b_col"]).then_inc(late_constants, 16)
                sp.dma_start(mask_q[:, :, :], a["mask"].rearrange("(t p) k -> p t k", p=P)).then_inc(late_constants, 16)
                sp.dma_start(mask_k[:, :, :], a["mask_T"].rearrange("(t p) q -> p t q", p=P)).then_inc(late_constants, 16)

                def stores(b, last):
                    u = 0
                    for kind, n, what in plan:
                        if kind == "xturn" and n == DC - 1:
                            sp.wait_ge(*xn_made.done(A, b, 0))
                            sp.dma_start(tok(x_dram[0], b), x_new[:, :, :]).then_inc(xn_stored.sem(0), 16)
                        if kind in ("key", "query"):
                            sp.wait_ge(*c_parts_made.done(A, b, u))
                            settle(sp, "sp")
                            j, o, (c0, cw) = splits[u]
                            dst = q_dram[0] if j == "q" else k_dram[kv_jobs[j][0].index]
                            dst = dst[bass.ds(b, 1), :, o * P:(o + 1) * P, c0:c0 + cw].rearrange("b a p t -> p (b a) t")
                            sp.dma_start(dst, c_parts[:, u % NCP, :, 0:cw]).then_inc(c_parts_stored.sem(u), 16)
                            if u < LOAD_PIECES and not last:
                                if u == 0:
                                    sp.wait_ge(*turned.done(A, b, n_turn - 1))
                                load_tokens(b + 1, u)
                            if LOAD_PIECES <= u < 2 * LOAD_PIECES:
                                if u == LOAD_PIECES:
                                    sp.wait_ge(*big_full.before(A, b, (len(plan) - 1) % 8))
                                load_raw(b, u - LOAD_PIECES)
                            u += 1
                        if kind == "value" and what is v_pairs[-1]:
                            sp.wait_ge(*v_made.done(A, b, (n + 1) * n_v - 1))
                            dst = v_dram[kv_jobs[n][0].index][bass.ds(b, 1)].rearrange("b g p e -> p (b g) e")
                            sp.dma_start(dst, v_stage[:, :].rearrange("p g t j e -> p g (t j e)")).then_inc(v_stored.sem(0), 16)
                with sp.Fori(0, B - 1) as b:
                    stores(b, False)
                stores(B - 1, True)
                sp.wait_ge(late_constants, 16 * n_late)
                sp.wait_ge(*xn_stored.done(A, B - 1, 0))
                sp.wait_ge(*v_stored.done(A, B - 1, 1))
                for u in range(len(splits) - NCP, len(splits)):
                    sp.wait_ge(*c_parts_stored.done(A, B - 1, u))

            @block.gpsimd
            def _(pool):
                nc.gpsimd.memset(ident[:, :], 0.0).then_inc(ident_made, 1)
                nc.gpsimd.memset(ident_b[:, :], 0.0).then_inc(ident_made, 1)
                pool.wait_ge(ident_made, 2)
                for m in (ident, ident_b):
                    nc.gpsimd.affine_select(out=m[:, :], in_=m[:, :], compare_op=ALU.not_equal, fill=1.0, base=0,
                                            pattern=[[-1, P]], channel_multiplier=1).then_inc(ident_made, 1)
                nc.gpsimd.memset(neg_half[:, :], -0.5).then_inc(consts_set, 1)
                nc.gpsimd.memset(v_stage[:, :], 1.0).then_inc(consts_set, 1)
                pool.wait_ge(constants, 16 * n_const)

                def norm_rstd(b):
                    pool.wait_ge(*norm_step.done(A, b, 3))
                    nc.gpsimd.tensor_tensor(rstd[:, :], spread[:, 1, :], neg_half[:, :], ALU.pow).then_inc(rstd_made.sem(0), 1)

                def body(b, last):
                    pool.wait_ge(*hat_made.done(A, b, NTT - 1))
                    pool.wait_ge(*xn_stored.before(A, b, 0))
                    nc.gpsimd.tensor_tensor(x_new[:, :, :], x_hat[:, :, :], row["L0_xattn_gq"].unsqueeze(1).broadcast_to([P, NQT, D]),
                                            ALU.mult).then_inc(xn_made.sem(0), 1)
                    for u in range(len(splits)):
                        cw = splits[u][2][1]
                        pool.wait_ge(*c_rest_made.done(A, b, u))
                        nc.gpsimd.tensor_tensor(c_parts[:, u % NCP, 2, 0:cw], c_proj[:, u % NCP, 0:cw], c_parts[:, u % NCP, 1, 0:cw],
                                                ALU.subtract).then_inc(c_parts_made.sem(u), 1)
                        if u == norm_use and not last:
                            norm_rstd(b + 1)

                pool.wait_ge(consts_set, 2)
                norm_rstd(0)
                pool.wait_ge(constants, 16 * n_const)
                with pool.Fori(0, B - 1) as b:
                    body(b, False)
                body(B - 1, True)

            @block.vector
            def _(dve):
                nc.vector.memset(mean_var[:, :, :], 1.0).then_inc(bias_made, 1)
                nc.vector.memset(o_ps, 0.0).then_inc(bias_made, 1)
                dve.wait_ge(bias_made, 2)
                tiles = [(t, c_tok[0:L0.rows[t], t, :], L0.rows[t]) for t in range(KVT)]
                tiles += [(KVT + t, x_res[:, t, :], P) for t in range(NQT)]

                def norm_statistics(b, some):
                    if some[0] is tiles[0]:
                        dve.wait_ge(*ctx_loaded.done(A, b, LOAD_PIECES))
                        dve.wait_ge(*xin_loaded.done(A, b, 0))
                    for t, src, r in some:
                        last = nc.vector.bn_stats(stats[0:r, t, :], src)
                    if some[-1] is not tiles[-1]:
                        return
                    last.then_inc(norm_step.sem(0), 1)
                    dve.wait_ge(*norm_step.done(A, b, 0))
                    settle(dve, "dve")
                    for t, src, r in tiles:
                        last = nc.vector.bn_aggr(mean_var[0:r, t, :], stats[0:r, t, :])
                    last.then_inc(norm_step.sem(0), 1)
                    dve.wait_ge(*norm_step.done(A, b, 1))
                    nc.vector.tensor_tensor(spread[:, 0, :], mean_var[:, :, 0], mean_var[:, :, 0], ALU.mult).then_inc(norm_step.sem(0), 1)
                    dve.wait_ge(*norm_step.done(A, b, 2))
                    nc.vector.scalar_tensor_tensor(out=spread[:, 1, :], in0=spread[:, 0, :], scalar=EPS_RMS, in1=mean_var[:, :, 1],
                                                   op0=ALU.add, op1=ALU.add).then_inc(norm_step.sem(0), 1)

                def norm_apply(b, some):
                    if some[0] is tiles[0]:
                        dve.wait_ge(*rstd_made.done(A, b, 0))
                        dve.wait_ge(*xn_made.before(A, b, 0))
                        dve.wait_ge(*turned.before(A, b, 0))
                    for t, src, r in some:
                        dst = src if t < KVT else x_hat[:, t - KVT, :]
                        nc.vector.tensor_scalar(dst, src, rstd[0:r, t:t + 1], None, ALU.mult).then_inc(hat_made.sem(0), 1)

                def body(b, last_batch):
                    u = 0
                    for k, (kind, n, what) in enumerate(plan):
                        if kind in ("key", "query"):
                            cw = splits[u][2][1]
                            f, p = c_proj[:, u % NCP, 0:cw], c_parts[:, u % NCP, :, 0:cw]
                            dve.wait_ge(*c_proj_made.done(A, b, u))
                            nc.vector.tensor_tensor(f, f, p[:, 0, :], ALU.subtract).then_inc(c_rest_step.sem(u), 1)
                            dve.wait_ge(*c_rest_step.done(A, b, u))
                            nc.vector.tensor_copy(p[:, 1, :], f).then_inc(c_rest_made.sem(u), 1)
                            n_apply = u - len(splits) // 2 - 2
                            if n_apply in range(4) and not last_batch:
                                norm_apply(b + 1, tiles[5 * n_apply:5 * n_apply + 5])
                            u += 1
                        if kind == "value":
                            bias = kv_jobs[n][4]
                            dve.wait_ge(*big_full.done(A, b, k))
                            if what is v_pairs[0]:
                                dve.wait_ge(*v_stored.before(A, b, n))
                            for i, t in enumerate(what):
                                r = L0.rows[t]
                                dst = staged(t, r)
                                src = by_head(psum[0:r, k % 8, i * D:(i + 1) * D])
                                if bias is None:
                                    last = nc.vector.tensor_copy(dst, src)
                                else:
                                    last = nc.vector.tensor_tensor(dst, src, by_head(bias[0:r]), ALU.add)
                                if i + 1 < len(what):
                                    continue
                                last.then_inc(v_made.sem(0), 1)
                            n_stat = v_pairs.index(what)
                            if n == 0 and not last_batch and tiles[3 * n_stat:]:
                                norm_statistics(b + 1, tiles[3 * n_stat:3 * n_stat + 3])

                norm_statistics(0, tiles)
                norm_apply(0, tiles)
                dve.wait_ge(constants, 16 * n_const)
                dve.wait_ge(consts_set, 2)
                with dve.Fori(0, B - 1) as b:
                    body(b, False)
                body(B - 1, True)
                dve.wait_ge(late_constants, 16 * n_late)
                for i, n in enumerate(("L1_xattn_q_b", "L1_xattn_cq_b")):
                    nc.vector.tensor_scalar(q_bias[:, i, :], col[n], SCALE, None, ALU.mult).then_inc(bias_made, 1)
                dve.wait_ge(bias_made, 4)
                rest = probs[:, 1].rearrange("p (t q) -> p t q", t=S // P)
                nc.vector.tensor_scalar(rest, mask_k[:, :, :], MASK_FLOOR, None, ALU.max).then_inc(mask_step, 1)
                for k in range(3):
                    dve.wait_ge(mask_step, 2 * k + 1)
                    nc.vector.tensor_copy(mask_parts[:, k], rest).then_inc(mask_step, 1)
                    dve.wait_ge(mask_step, 2 * k + 2)
                    if k < 2:
                        nc.vector.tensor_tensor(rest, rest, mask_parts[:, k], ALU.subtract).then_inc(mask_step, 1)

            @block.scalar
            def _(act):
                act.wait_ge(constants, 16 * n_const)
                with act.Fori(0, B) as b:
                    u = 0
                    for k, (kind, n, what) in enumerate(plan):
                        bank = psum[:, k % 8]
                        if kind in ("turn", "xturn"):
                            act.wait_ge(*big_full.done(A, b, k))
                        if kind == "turn":
                            t0, t1 = what[0] * P, min(what[-1] * P + P, KV)
                            nc.scalar.activation(c_norm[:, n, t0:t1], bank[:, 0:t1 - t0], ACT.Copy,
                                                 scale=col["L0_xattn_gkv"][:, n:n + 1]).then_inc(turned.sem(0), 1)
                        if kind == "xturn":
                            nc.scalar.activation(hT[:, n, :], bank[:, :], ACT.Copy,
                                                 scale=col["L0_xattn_gq"][:, n:n + 1]).then_inc(turned.sem(0), 1)
                        if kind in ("key", "query"):
                            cw = splits[u][2][1]
                            act.wait_ge(*big_full.done(A, b, k))
                            act.wait_ge(*c_parts_stored.before(A, b, u))
                            scale = SCALE if kind == "query" else 1.0
                            nc.scalar.activation(c_proj[:, u % NCP, 0:cw], bank[:, 0:cw], ACT.Copy, scale=scale)
                            nc.scalar.activation(c_parts[:, u % NCP, 0, 0:cw], bank[:, 0:cw], ACT.Copy, scale=scale).then_inc(c_proj_made.sem(u), 1)
                            u += 1

            @block.tensor
            def _(pe):
                pe.wait_ge(constants, 16 * n_const)
                pe.wait_ge(ident_made, 4)

                def body(b, before):
                    for k, (kind, n, what) in enumerate(plan):
                        bank = psum[:, k % 8]
                        if k < 8 and before is not None:
                            signal, use = reader[max(range(k, len(plan), 8))]
                            pe.wait_ge(*signal.done(A, before, use))
                        if k >= 8:
                            signal, use = reader[k - 8]
                            pe.wait_ge(*signal.done(A, b, use))
                        if kind == "turn":
                            pe.wait_ge(*hat_made.done(A, b, what[-1]))
                            for i, t in enumerate(what):
                                r = L0.rows[t]
                                last = nc.tensor.transpose(bank[:, i * P:i * P + r], c_tok[0:r, t, n * P:(n + 1) * P], ident[0:r, 0:r])
                        if kind == "xturn":
                            pe.wait_ge(*hat_made.done(A, b, NTT - 1))
                            for t in range(NQT):
                                last = nc.tensor.transpose(bank[:, t * P:(t + 1) * P], x_hat[:, t, n * P:(n + 1) * P], ident[:, :])
                        if kind == "key" and what == (0, L0.chunks[0]):
                            if n == 0:
                                pe.wait_ge(*turned.done(A, b, DC * len(t_groups) - 1))
                            else:
                                pe.wait_ge(*raw_loaded.done(A, b, LOAD_PIECES - 1))
                        if kind == "query" and n == 0:
                            pe.wait_ge(*turned.done(A, b, n_turn - 1))
                        if kind == "key":
                            o, (c0, cw) = what
                            for c in range(DC):
                                last = nc.tensor.matmul(bank[:, 0:cw], kv_jobs[n][1][:, c, o * P:(o + 1) * P],
                                                        kv_jobs[n][3][:, c, c0:c0 + cw], start=c == 0, stop=c == DC - 1)
                        if kind == "query":
                            for c in range(DC):
                                last = nc.tensor.matmul(bank[:, :], w["L0_xattn_wq"][:, c, n * P:(n + 1) * P], hT[:, c, :],
                                                        start=c == 0, stop=c == DC - 1)
                        if kind == "value":
                            for i, t in enumerate(what):
                                r = L0.rows[t]
                                for c in range(DC):
                                    last = nc.tensor.matmul(bank[0:r, i * D:(i + 1) * D], kv_jobs[n][3][:, c, t * P:t * P + r],
                                                            kv_jobs[n][2][:, c, :], start=c == 0, stop=c == DC - 1)
                        last.then_inc(big_full.sem(k), 1)

                body(0, None)
                with pe.Fori(0, B - 1) as before:
                    body(before + 1, before)

        n_split = {"L0": 4, "self": 2, "cross": 0}
        for st in STAGES:
            for c, uses in ((group_loaded, NG), (max_rows_loaded, NG), (s_full, GH * st.steps),
                            (masked_done, len(DVE_MASKED) * st.steps * st.masked),
                            (exp_done, GH * st.steps), (pv_done, st.steps), (m_full, NG * st.max_uses),
                            (m_free, NG * st.max_uses), (max_step, NG), (max_first, NG), (max_rest, NG), (max_second, NG), (max_ready, NG),
                            (o_moved, NG), (recip_made, NG),
                            (res_loaded, 1), (res_made, 1), (x_stored, 1), (t_step, 3), (t_rstd, 1), (t_hat, NQT),
                            (h_stored, st is CROSS), (proj_made, n_split[st.name]), (rest_step, n_split[st.name]),
                            (rest_made, n_split[st.name]), (parts_made, n_split[st.name]), (parts_stored, n_split[st.name]),
                            (v_stored, st is L0)):
                c.plan(st.name, int(uses))
        for c in (small_full, small_free):
            c.plan("start", 1, 1)
            for st in STAGES:
                for kind, times in (("first", 1), ("mid", B - 2), ("last", 1)):
                    c.plan(f"{st.name} {kind}", len(Body(st, kind).order), times)
            c.plan(f"{CROSS.name} end", len(Body(CROSS, "end").order), 1)

        def small_at(count, body, item, done):
            use = body.order.index(item)
            return (count.done if done else count.before)(body.name, body.r, use)

        out_w = {"L0": w["L0_xattn_wo"], "self": w["L1_xattn_o_w"], "cross": w["L1_xattn_co_w"]}
        out_b = {"L0": row["L0_xattn_bo"], "self": row["L1_xattn_o_b"], "cross": row["L1_xattn_co_b"]}
        ln_w = {"L0": col["L1_xattn_attn_ln_w"], "self": col["L1_xattn_cross_ln_w"], "cross": col["L1_xattn_mlp_ln_w"]}
        ln_b = {"L0": col["L1_xattn_attn_ln_b"], "self": col["L1_xattn_cross_ln_b"], "cross": col["L1_xattn_mlp_ln_b"]}
        q_w = {"L0": w["L1_xattn_q_w"], "self": w["L1_xattn_cq_w"]}
        q_b = {"L0": q_bias[:, 0, :], "self": q_bias[:, 1, :]}
        k_w, v_w = w["L1_xattn_k_w"], w["L1_xattn_v_w"]

        def tail_splits(st):
            return [x for x in st.tail if x[0] in "qk"]

        def bodies(eng, body):
            for st in STAGES:
                body(Body(st, "first"))
                with eng.Fori(0, B - 2) as r:
                    body(Body(st, "mid", r))
                body(Body(st, "last"))
            body(Body(CROSS, "end"))

        def steps(body):
            return range(1 if body.kind == "end" else body.st.steps)

        with nc.Block() as block:
            @block.sync
            def _(sp):
                def load_group(st, b, k):
                    g = k

                    def heads(dr, part):
                        src = dr[bass.ds(b, 1), part, g * GW:(g + 1) * GW, :]
                        return src.rearrange("b (h d) t -> (b d) h t", d=DH)
                    loaded = group_loaded.sem(k)
                    for i, (kp, qp) in enumerate(zip(K_PARTS, Q_PARTS)):
                        r0, r1 = i * DH, (i + 1) * DH
                        sp.dma_start(queries[r0:r1, g, :, :], heads(q_dram[st.index], qp)).then_inc(loaded, 16)
                        sp.dma_start(keys[r0:r1, g, :, 0:st.keys], heads(k_dram[st.index], kp)).then_inc(loaded, 16)
                    src = v_dram[st.index][bass.ds(b, 1), g].rearrange("b p e -> (b p) e")
                    sp.dma_start(values[:, g, 0:st.KT].rearrange("p t j e -> p (t j e)"), src).then_inc(loaded, 16)

                def load_max_rows(g, moved):
                    sp.wait_ge(*moved)
                    for i in range(MR):
                        n = MAX_ROWS
                        d = queries[PR + i:PR + i + 1, g, :, :]
                        dst = bass.AP(tensor=d.tensor, offset=d.offset, ap=[list(d.ap[0]), [P, n], [1, P]])
                        s = max_rows[i * n:(i + 1) * n, :]
                        sp.dma_start(dst, s).then_inc(max_rows_loaded.sem(g), 16)

                def stores_done(st, b, all_of_b):
                    at = Count.done if all_of_b else Count.before
                    sp.wait_ge(*at(x_stored, st.name, b, 0))
                    for u in range(len(tail_splits(st)))[-2:]:
                        sp.wait_ge(*(parts_stored.done(st.name, b, u) if all_of_b else parts_stored.before(st.name, b, u % 2)))
                    if st is L0:
                        sp.wait_ge(*at(v_stored, st.name, b, 0))
                    if st is CROSS:
                        sp.wait_ge(*at(h_stored, st.name, b, 0))

                def store_tail(body, item):
                    st, b = body.tail_st, body.tail_b
                    if item == "out1":
                        sp.wait_ge(*small_at(small_free, body, ("tail", item), True))
                        sp.dma_start(tok(x_dram[st.index + 1], b), x_new[:, :, :]).then_inc(x_stored.sem(0), 16)
                    if item == "hT1" and st is CROSS:
                        sp.wait_ge(*small_at(small_free, body, ("tail", item), True))
                        sp.dma_start(h_dram[bass.ds(b, 1)].rearrange("b p e -> (b p) e"),
                                     hT[:, :, :].rearrange("p c t -> p (c t)")).then_inc(h_stored.sem(0), 16)
                    if item in tail_splits(st):
                        u, o = tail_splits(st).index(item), int(item[1])
                        dr = q_dram[st.index + 1] if item[0] == "q" else k_dram[st.index + 1]
                        sp.wait_ge(*parts_made.done(st.name, b, u))
                        settle(sp, "sp")
                        dst = dr[bass.ds(b, 1), :, o * P:(o + 1) * P, :].rearrange("b a p t -> p (b a) t")
                        sp.dma_start(dst, parts[:, u % 2, :, :]).then_inc(parts_stored.sem(u), 16)
                    if item == "v1":
                        sp.wait_ge(*small_at(small_free, body, ("tail", item), True))
                        dst = v_dram[1][bass.ds(b, 1)].rearrange("b g p e -> p (b g) e")
                        sp.dma_start(dst, v_stage[:, :, 0:NQT].rearrange("p g t j e -> p g (t j e)")).then_inc(v_stored.sem(0), 16)

                for k in range(3):
                    load_group(L0, 0, k)
                load_max_rows(0, small_free.done("start", 0, 0))

                def body(bd):
                    st, KT = bd.st, bd.st.KT
                    if bd.tail_st is not None:
                        sp.wait_ge(*t_step.before(bd.tail_st.name, bd.tail_b, 0))
                        sp.dma_start(x_res[:, :, :], tok(x_dram[bd.tail_st.index], bd.tail_b)).then_inc(res_loaded.sem(0), 16)
                    if bd.kind == "first" and bd.tail_st is not None:
                        stores_done(bd.tail_st, B - 1, False)
                    for i in steps(bd):
                        g, t = divmod(i, KT)
                        to = bd.following(g + 3) if bd.kind != "end" else None
                        if t == 1 and to:
                            if g:
                                sp.wait_ge(*pv_done.done(st.name, bd.b, g * KT - 1))
                            elif bd.kind == "first" and bd.tail_st is not None:
                                sp.wait_ge(*pv_done.done(bd.tail_st.name, B - 1, bd.tail_st.steps - 1))
                            else:
                                sp.wait_ge(*pv_done.before(st.name, bd.b, (st.steps - 1) % NP))
                            if to[0] is not st and g == 1:
                                stores_done(st, B - 2, False)
                            load_group(*to)
                        for kind, item in bd.small[i]:
                            if kind == "tail":
                                store_tail(bd, item)
                            if kind == "max":
                                load_max_rows(item % NG, small_at(small_free, bd, (kind, item), True))
                    if bd.kind == "first" and bd.tail_st is not None:
                        stores_done(bd.tail_st, B - 1, True)
                    if bd.kind == "first" and st is CROSS:
                        sp.dma_start(fc1, a["L1_xattn_fc1_w"].rearrange("(c p) f -> p c f", p=P)).then_inc(fc_loaded, 16)
                        sp.dma_start(fc2, a["L1_xattn_fc2_w"].rearrange("(c p) d -> p c d", p=P)).then_inc(fc_loaded, 16)
                    if bd.kind == "end":
                        stores_done(CROSS, B - 1, True)

                bodies(sp, body)

            @block.gpsimd
            def _(pool):
                for g in range(NG):
                    words = keys_flat[PR:PR + MR, g * GH * KV:(g + 1) * GH * KV].bitcast(F32)
                    nc.gpsimd.memset(words, BF16_ONES).then_inc(ones_set, 1)
                pool.wait_ge(ones_set, NG)

                def body(bd):
                    st, b = bd.tail_st, bd.tail_b
                    if st is None:
                        return
                    pool.wait_ge(*res_loaded.done(st.name, b, 0))
                    nc.gpsimd.tensor_tensor(x_res[:, :, :], x_res[:, :, :], out_b[st.name].unsqueeze(1).broadcast_to([P, NQT, D]),
                                            ALU.add).then_inc(res_made.sem(0), 1)
                    pool.wait_ge(*t_step.done(st.name, b, 2))
                    nc.gpsimd.tensor_tensor(rstd[:, 0:NQT], spread[:, 0, 0:NQT], neg_half[:, 0:NQT], ALU.pow).then_inc(t_rstd.sem(0), 1)
                    for u in range(len(tail_splits(st))):
                        pool.wait_ge(*rest_made.done(st.name, b, u))
                        nc.gpsimd.tensor_tensor(parts[:, u % 2, 2, :], proj[:, u % 2, :], parts[:, u % 2, 1, :],
                                                ALU.subtract).then_inc(parts_made.sem(u), 1)

                bodies(pool, body)

            @block.tensor
            def _(pe):
                def group_maxima(to, some):
                    if not some:
                        return
                    st, b, k = to
                    g = k
                    if some[0] == 0:
                        pe.wait_ge(*group_loaded.done(st.name, b, k))
                    for n in some:
                        r, c = divmod(n, st.NCH)
                        j, qt = divmod(r, NQT)
                        c0, cw = st.chunks[c]
                        use = k * st.max_uses + n
                        pe.wait_ge(*m_free.before(st.name, b, use))
                        nc.tensor.matmul(m_ps[:, use % MB, 0:cw], queries[0:PR, g, j, qt * P:(qt + 1) * P],
                                         keys[0:PR, g, j, c0:c0 + cw], start=True, stop=True).then_inc(m_full.sem(use), 1)

                def turn_maxima(to, before):
                    pe.wait_ge(*before)
                    pe.wait_ge(*max_ready.done(to[0].name, to[1], to[2]))
                    nc.tensor.matmul(small[0:MR * MAX_ROWS, 0:P], max_parts[:, :], ident_b[:, :],
                                     start=True, stop=True).then_inc(small_full.sem(0), 1)

                def scores(st, b, i, heads):
                    g, t = divmod(i, st.KT)
                    r = st.rows[t]
                    if t == 0 and heads[0] == 0:
                        pe.wait_ge(*max_rows_loaded.done(st.name, b, g))
                    for j in heads:
                        use = GH * i + j
                        pe.wait_ge(*exp_done.before(st.name, b, use))
                        with_mask = st.masked and j not in DVE_MASKED
                        mm = nc.tensor.matmul(s_ps[0:r, use % SB, :], keys[0:PR + MR, g, j, t * P:t * P + r],
                                              queries[0:PR + MR, g, j, :], start=True, stop=not with_mask)
                        if with_mask:
                            for k in range(3):
                                mm = nc.tensor.matmul(s_ps[:, use % SB, :], ident_b[:, :], mask_parts[:, k, t, :],
                                                      start=False, stop=k == 2)
                        mm.then_inc(s_full.sem(use), 1)

                def weighted_sums(st, b, i):
                    g, t = divmod(i, st.KT)
                    r = st.rows[t]
                    for j in range(GH):
                        pe.wait_ge(*exp_done.done(st.name, b, GH * i + j))
                    if t == 0:
                        pe.wait_ge(*o_moved.before(st.name, b, g))
                    for j in range(GH):
                        last = nc.tensor.matmul(o_ps[32 * j:32 * j + VH, :], values[0:r, g, t, j, :],
                                                probs[0:r, i % NP, j * S:(j + 1) * S], start=t == 0, stop=t == st.KT - 1,
                                                tile_position=(0, 32 * j), skip_group_check=True)
                    last.then_inc(pv_done.sem(i), 1)

                def turn_sums(bd, item, st, b, g):
                    pe.wait_ge(*small_at(small_free, bd, item, False))
                    pe.wait_ge(*o_moved.done(st.name, b, g))
                    for t in range(NQT):
                        mm = nc.tensor.transpose(small[:, t * P:(t + 1) * P], o_sum[:, t * P:(t + 1) * P], ident[:, :])
                    mm.then_inc(small_full.sem(0), 1)

                def tail(bd, what):
                    st, b = bd.tail_st, bd.tail_b
                    if what == "turn3":
                        turn_sums(bd, ("tail", what), st, b, NG - 1)
                        return
                    c = int(what[-1])
                    pe.wait_ge(*small_at(small_free, bd, ("tail", what), False))
                    if what[:2] == "oT":
                        for t in range(NQT):
                            mm = nc.tensor.transpose(small[:, t * P:(t + 1) * P], o_tok[:, t, c * P:(c + 1) * P], ident[:, :])
                    if what[:2] == "hT":
                        for t in range(NQT):
                            pe.wait_ge(*t_hat.done(st.name, b, t))
                            mm = nc.tensor.transpose(small[:, t * P:(t + 1) * P], x_hat[:, t, c * P:(c + 1) * P], ident[:, :])
                    if what[0] in "qk":
                        wt = q_w[st.name] if what[0] == "q" else k_w
                        for n in range(DC):
                            mm = nc.tensor.matmul(small[:, :], wt[:, n, c * P:(c + 1) * P], hT[:, n, :],
                                                  start=n == 0, stop=n == DC - 1)
                    if what[:3] == "out" or what[0] == "v":
                        src, wt = (oT, out_w[st.name]) if what[0] == "o" else (hT, v_w)
                        for i in range(2):
                            t = 2 * c + i
                            for n in range(DC):
                                mm = nc.tensor.matmul(small[:, i * D:(i + 1) * D], src[:, n, t * P:(t + 1) * P], wt[:, n, :],
                                                      start=n == 0, stop=n == DC - 1)
                    mm.then_inc(small_full.sem(0), 1)

                first = (L0, 0, 0)
                group_maxima(first, range(L0.max_uses))
                turn_maxima(first, small_free.before("start", 0, 0))
                pe.wait_ge(ones_set, NG)

                def body(bd):
                    for i in steps(bd):
                        to, some = bd.share(i)
                        for what, n in ORDER:
                            if what == "scores" and bd.kind != "end":
                                scores(bd.st, bd.b, i, (n,))
                            if what == "maxima":
                                group_maxima(to, cut(some, n))
                            if what == "sums" and i:
                                weighted_sums(bd.st, bd.b, i - 1)
                            if what == "sums" and not i and bd.tail_st is not None:
                                weighted_sums(bd.tail_st, bd.tail_b, bd.tail_st.steps - 1)
                        for kind, item in bd.small[i]:
                            if kind == "tail":
                                tail(bd, item)
                            if kind == "turn":
                                turn_sums(bd, (kind, item), bd.st, bd.b, item)
                            if kind == "max":
                                turn_maxima(bd.following(item), small_at(small_free, bd, (kind, item), False))

                bodies(pe, body)

            @block.scalar
            def _(act):
                def exps(st, b, i, heads):
                    r = st.rows[i % st.KT]
                    if heads[0] == 0:
                        act.wait_ge(*pv_done.before(st.name, b, i))
                    for j in heads:
                        use = GH * i + j
                        if st.masked and j in DVE_MASKED:
                            act.wait_ge(*masked_done.done(st.name, b, len(DVE_MASKED) * i + DVE_MASKED.index(j)))
                        else:
                            act.wait_ge(*s_full.done(st.name, b, use))
                        nc.scalar.activation(probs[0:r, i % NP, j * S:(j + 1) * S], s_ps[0:r, use % SB, :],
                                             ACT.Exp).then_inc(exp_done.sem(use), 1)

                def move_sums(bd, st, b, g, turned_before):
                    act.wait_ge(*pv_done.done(st.name, b, (g + 1) * st.KT - 1))
                    if turned_before:
                        act.wait_ge(*turned_before)
                    nc.scalar.activation(o_sum[:, :], o_ps[:, :], ACT.Copy).then_inc(o_moved.sem(0), 1)

                def tail(bd, what):
                    st, b = bd.tail_st, bd.tail_b
                    if what[:2] not in ("oT", "hT") and what[0] not in "qk":
                        return
                    c = int(what[-1])
                    act.wait_ge(*small_at(small_full, bd, ("tail", what), True))
                    if what[:2] == "oT":
                        mv = nc.scalar.activation(oT[:, c, :], small[:, :], ACT.Copy)
                    if what[:2] == "hT":
                        if st is CROSS and c == 0:
                            act.wait_ge(*h_stored.before(st.name, b, 0))
                        mv = nc.scalar.activation(hT[:, c, :], small[:, :], ACT.Identity, bias=ln_b[st.name][:, c:c + 1],
                                                  scale=ln_w[st.name][:, c:c + 1])
                    if what[0] in "qk":
                        u = tail_splits(st).index(what)
                        act.wait_ge(*parts_stored.before(st.name, b, u))
                        for dst in (proj[:, u % 2, :], parts[:, u % 2, 0, :]):
                            if what[0] == "q":
                                mv = nc.scalar.activation(dst, small[:, :], ACT.Identity, bias=q_b[st.name][:, c:c + 1], scale=SCALE)
                            else:
                                mv = nc.scalar.activation(dst, small[:, :], ACT.Copy)
                    mv.then_inc(small_free.sem(0), 1)

                def body(bd):
                    def tails(items):
                        for kind, item in items:
                            if kind == "tail":
                                tail(bd, item)

                    for i in steps(bd):
                        g, t = divmod(i, bd.st.KT)
                        if bd.kind != "end":
                            exps(bd.st, bd.b, i, (0, 1))
                        if i:
                            tails(bd.small[i - 1][-1:])
                        if bd.kind != "end":
                            exps(bd.st, bd.b, i, (2, 3))
                        if i and t == 0:
                            before = ("turn", g - 2) if g > 1 else ("tail", "turn3")
                            move_sums(bd, bd.st, bd.b, g - 1, before in bd.order and small_at(small_full, bd, before, True))
                        if i == 0 and bd.tail_st is not None:
                            move_sums(bd, bd.tail_st, bd.tail_b, NG - 1, small_full.before(bd.name, bd.r, 0))
                        tails(bd.small[i][:-1])
                    tails(bd.small[i][-1:])

                bodies(act, body)

            @block.vector
            def _(dve):
                def group_maxima(to, some):
                    for n in some:
                        st, b, k = to
                        r, c = divmod(n, st.NCH)
                        c0, cw = st.chunks[c]
                        use = k * st.max_uses + n
                        dve.wait_ge(*m_full.done(st.name, b, use))
                        dst = part_max[:, n:n + 1]
                        if st.masked:
                            settle(dve, "dve")
                            op = nc.vector.tensor_tensor_reduce(junk[use % MB][:, 0:cw], m_ps[:, use % MB, 0:cw],
                                                                mask_q[:, r % NQT, c0:c0 + cw], 1.0, LOWEST, ALU.add, ALU.max, dst)
                        else:
                            op = nc.vector.tensor_reduce(dst, m_ps[:, use % MB, 0:cw], AX.X, ALU.max)
                        op.then_inc(m_free.sem(use), 1)

                def split_maxima(to):
                    st, b, k = to
                    end = (k + 1) * st.max_uses
                    for use in range(end - MB, end):
                        dve.wait_ge(*m_free.done(st.name, b, use))
                    n = MAX_ROWS
                    nc.vector.tensor_reduce(neg_max[:, :], part_max[:, 0:st.max_uses].rearrange("p (r c) -> p r c", c=st.NCH),
                                            AX.X, ALU.max, negate=True).then_inc(max_step.sem(0), 1)
                    dve.wait_ge(*max_step.done(st.name, b, k))
                    nc.vector.tensor_copy(max_parts[:, 0:n], neg_max[:, :]).then_inc(max_first.sem(0), 1)
                    dve.wait_ge(*max_first.done(st.name, b, k))
                    nc.vector.tensor_tensor(neg_max[:, :], neg_max[:, :], max_parts[:, 0:n], ALU.subtract).then_inc(max_rest.sem(0), 1)
                    dve.wait_ge(*max_rest.done(st.name, b, k))
                    nc.vector.tensor_copy(max_parts[:, n:2 * n], neg_max[:, :]).then_inc(max_second.sem(0), 1)
                    dve.wait_ge(*max_second.done(st.name, b, k))
                    nc.vector.tensor_tensor(max_parts[:, 2 * n:3 * n], neg_max[:, :], max_parts[:, n:2 * n],
                                            ALU.subtract).then_inc(max_ready.sem(0), 1)

                def move_maxima(full):
                    dve.wait_ge(*full)
                    nc.vector.tensor_copy(max_rows[:, :], small[0:MR * MAX_ROWS, 0:P]).then_inc(small_free.sem(0), 1)

                def add_mask(st, b, i, heads):
                    for j in heads:
                        use = GH * i + j
                        dve.wait_ge(*s_full.done(st.name, b, use))
                        nc.vector.tensor_tensor(s_ps[:, use % SB], s_ps[:, use % SB], mask_k[:, i % st.KT, :],
                                                ALU.add).then_inc(masked_done.sem(len(DVE_MASKED) * i + DVE_MASKED.index(j)), 1)

                def normalize(bd, item, st, b, g):
                    dve.wait_ge(*small_at(small_full, bd, item, True))
                    v = small[:, :].rearrange("p (t j r) -> p t j r", t=NQT, j=GH)
                    nc.vector.reciprocal(recip[:, :, :], v[:, :, :, DH]).then_inc(recip_made.sem(0), 1)
                    dve.wait_ge(*recip_made.done(st.name, b, g))
                    dst = o_tok[:, :, g * GW:(g + 1) * GW].rearrange("p t (j d) -> p t j d", j=GH)
                    nc.vector.tensor_tensor(dst, v[:, :, :, 0:DH], recip[:, :, :].unsqueeze(3).broadcast_to([P, NQT, GH, DH]),
                                            ALU.mult).then_inc(small_free.sem(0), 1)

                def norm_statistics(bd, t):
                    st, b = bd.tail_st, bd.tail_b
                    if t % 2 == 0:
                        dve.wait_ge(*small_at(small_free, bd, ("tail", f"out{t // 2}"), True))
                    op = nc.vector.bn_stats(stats[:, t, :], x_new[:, t, :])
                    if t < NQT - 1:
                        return
                    op.then_inc(t_step.sem(0), 1)
                    dve.wait_ge(*t_step.done(st.name, b, 0))
                    settle(dve, "dve")
                    for t in range(NQT):
                        op = nc.vector.bn_aggr(mean_var[:, t, :], stats[:, t, :])
                    op.then_inc(t_step.sem(0), 1)
                    dve.wait_ge(*t_step.done(st.name, b, 1))
                    nc.vector.tensor_scalar(spread[:, 0, 0:NQT], mean_var[:, 0:NQT, 1], EPS_LN, None, ALU.add).then_inc(t_step.sem(0), 1)

                def norm_apply(bd, t):
                    st, b = bd.tail_st, bd.tail_b
                    if t == 0:
                        dve.wait_ge(*t_rstd.done(st.name, b, 0))
                    nc.vector.tensor_scalar(x_hat[:, t, :], x_new[:, t, :], mean_var[:, t, 0:1], rstd[:, t:t + 1],
                                            ALU.subtract, ALU.mult).then_inc(t_hat.sem(0), 1)

                def tail(bd, what):
                    st, b = bd.tail_st, bd.tail_b
                    if what == "turn3":
                        normalize(bd, ("tail", what), st, b, NG - 1)
                    if what[:3] == "out":
                        t = 2 * int(what[-1])
                        if t == 0:
                            dve.wait_ge(*res_made.done(st.name, b, 0))
                            dve.wait_ge(*x_stored.before(st.name, b, 0))
                        dve.wait_ge(*small_at(small_full, bd, ("tail", what), True))
                        nc.vector.tensor_tensor(x_new[:, t:t + 2, :], small[:, :].rearrange("p (t d) -> p t d", t=2), x_res[:, t:t + 2, :],
                                                ALU.add).then_inc(small_free.sem(0), 1)
                        if bd.kind == "end":
                            norm_statistics(bd, t)
                            norm_statistics(bd, t + 1)
                        if bd.kind == "end" and t:
                            for t in range(NQT):
                                norm_apply(bd, t)
                    if what[0] in "qk":
                        u = tail_splits(st).index(what)
                        f, p = proj[:, u % 2, :], parts[:, u % 2]
                        dve.wait_ge(*small_at(small_free, bd, ("tail", what), True))
                        nc.vector.tensor_tensor(f, f, p[:, 0, :], ALU.subtract).then_inc(rest_step.sem(u), 1)
                        dve.wait_ge(*rest_step.done(st.name, b, u))
                        nc.vector.tensor_copy(p[:, 1, :], f).then_inc(rest_made.sem(u), 1)
                    if what[0] == "v":
                        t = 2 * int(what[-1])
                        if t == 0:
                            dve.wait_ge(*v_stored.before(st.name, b, 0))
                        dve.wait_ge(*small_at(small_full, bd, ("tail", what), True))
                        for i in range(2):
                            op = nc.vector.tensor_tensor(staged(t + i), by_head(small[:, i * D:(i + 1) * D]),
                                                         by_head(row["L1_xattn_v_b"]), ALU.add)
                        op.then_inc(small_free.sem(0), 1)

                first = (L0, 0, 0)
                group_maxima(first, range(L0.max_uses))
                split_maxima(first)
                move_maxima(small_full.done("start", 0, 0))

                def body(bd):
                    def use_small(items):
                        for kind, item in items:
                            if kind == "tail":
                                tail(bd, item)
                            if kind == "turn":
                                normalize(bd, (kind, item), bd.st, bd.b, item)
                            if kind == "max":
                                move_maxima(small_at(small_full, bd, (kind, item), True))

                    rests = tail_splits(bd.tail_st) if bd.tail_st is not None else []
                    for i in steps(bd):
                        to, some = bd.share(i)
                        for what, n in ORDER:
                            if what == "scores" and bd.st.masked and bd.kind != "end" and n in DVE_MASKED:
                                add_mask(bd.st, bd.b, i, (n,))
                            if what == "maxima":
                                group_maxima(to, cut(some, n))
                            if what != "maxima" or bd.kind == "end":
                                continue
                            if i and n == READ_AFTER:
                                use_small([x for x in bd.small[i - 1][-1:] if x[1] not in rests])
                            if i and n == REST_AFTER:
                                use_small([x for x in bd.small[i - 1][-1:] if x[1] in rests])
                            if bd.tail_st is None:
                                continue
                            if n >= 2 and i == bd.step_of(("tail", "out0")) + 1:
                                norm_statistics(bd, n - 2)
                            if n >= 2 and i == bd.step_of(("tail", "out1")) + 1:
                                norm_statistics(bd, n)
                            if i == bd.step_of(("tail", "out1")) + 2:
                                norm_apply(bd, n)
                        if some and some[-1] == to[0].max_uses - 1:
                            split_maxima(to)
                        use_small(bd.small[i][:-1])
                    use_small(bd.small[i][-1:])

                bodies(dve, body)

        M = "mlp"
        N_F = FC + NQT // 2

        def f_bank(m):
            return (m + NQT // 2) % 8

        for c, uses in ((h_loaded, 1), (res_loaded, 1), (res_made, 1), (x_stored, 1), (f_full, N_F), (gelu_done, FC),
                        (y_made, NQT // 2)):
            c.plan(M, uses)

        with nc.Block() as block:
            @block.sync
            def _(sp):
                def load_h(b):
                    sp.dma_start(hT[:, :, :].rearrange("p c t -> p (c t)"),
                                 h_dram[bass.ds(b, 1)].rearrange("b p e -> (b p) e")).then_inc(h_loaded.sem(0), 16)

                def load_x(b):
                    sp.dma_start(x_res[:, :, :], tok(x_dram[3], b)).then_inc(res_loaded.sem(0), 16)

                load_h(0)
                load_x(0)

                def body(b, last):
                    if not last:
                        sp.wait_ge(*f_full.done(M, b, FC - 1))
                        load_h(b + 1)
                    sp.wait_ge(*y_made.done(M, b, NQT // 2 - 1))
                    sp.dma_start(tok(out, b), x_new[:, :, :]).then_inc(x_stored.sem(0), 16)
                    if not last:
                        load_x(b + 1)

                with sp.Fori(0, B - 1) as b:
                    body(b, False)
                body(B - 1, True)
                sp.wait_ge(*x_stored.done(M, B - 1, 0))

            @block.gpsimd
            def _(pool):
                with pool.Fori(0, B) as b:
                    pool.wait_ge(*res_loaded.done(M, b, 0))
                    nc.gpsimd.tensor_tensor(x_res[:, :, :], x_res[:, :, :], row["L1_xattn_fc2_b"].unsqueeze(1).broadcast_to([P, NQT, D]),
                                            ALU.add).then_inc(res_made.sem(0), 1)

            @block.tensor
            def _(pe):
                pe.wait_ge(fc_loaded, 32)
                with pe.Fori(0, B) as b:
                    pe.wait_ge(*h_loaded.done(M, b, 0))
                    for m in range(FC):
                        pe.wait_ge(*gelu_done.before(M, b, 0))
                        if f_bank(m) < NQT // 2:
                            pe.wait_ge(*y_made.before(M, b, 0))
                        for c in range(DC):
                            last = nc.tensor.matmul(psum[:, f_bank(m)], fc1[:, c, m * P:(m + 1) * P], hT[:, c, :], start=c == 0, stop=c == DC - 1)
                        last.then_inc(f_full.sem(m), 1)
                    for y in range(NQT // 2):
                        pe.wait_ge(*gelu_done.done(M, b, FC - 1))
                        for i in range(2):
                            t = 2 * y + i
                            for m in range(FC):
                                last = nc.tensor.matmul(psum[:, y, i * D:(i + 1) * D], h1[:, m, t * P:(t + 1) * P], fc2[:, m, :],
                                                        start=m == 0, stop=m == FC - 1)
                        last.then_inc(f_full.sem(FC + y), 1)

            @block.scalar
            def _(act):
                with act.Fori(0, B) as b:
                    for m in range(FC):
                        act.wait_ge(*f_full.done(M, b, m))
                        nc.scalar.activation(h1[:, m, :], psum[:, f_bank(m)], ACT.Gelu, bias=fc1_b[:, m:m + 1]).then_inc(gelu_done.sem(0), 1)

            @block.vector
            def _(dve):
                with dve.Fori(0, B) as b:
                    dve.wait_ge(*res_made.done(M, b, 0))
                    dve.wait_ge(*x_stored.before(M, b, 0))
                    for y in range(NQT // 2):
                        dve.wait_ge(*f_full.done(M, b, FC + y))
                        nc.vector.tensor_tensor(x_new[:, 2 * y:2 * y + 2, :], psum[:, y].rearrange("p (t d) -> p t d", t=2),
                                                x_res[:, 2 * y:2 * y + 2, :], ALU.add).then_inc(y_made.sem(0), 1)


_TURNED = [n for n in (
    "L0_xattn_wq", "L0_xattn_wk", "L0_xattn_wv", "L0_xattn_wo", "L1_xattn_q_w", "L1_xattn_k_w", "L1_xattn_v_w",
    "L1_xattn_o_w", "L1_xattn_cq_w", "L1_xattn_ck_w", "L1_xattn_cv_w", "L1_xattn_co_w", "L1_xattn_fc1_w", "L1_xattn_fc2_w")]


def kernel(**inputs):
    import numpy as np
    import concourse.bacc as bacc
    from concourse.bass_utils import run_bass_kernel_spmd

    laid = {}
    for name, value in inputs.items():
        value = np.asarray(value)
        if name in _TURNED:
            laid[name] = np.ascontiguousarray(value.T)
        elif name == "ctx_1024":
            laid["ctx"] = np.ascontiguousarray(value)
            laid["ctx_T"] = np.ascontiguousarray(value.transpose(0, 2, 1))
        elif name == "mask_SxS_fc0":
            laid["mask"] = np.ascontiguousarray(value)
            laid["mask_T"] = np.ascontiguousarray(value.T)
        elif name in ROW_NAMES or name == "x":
            laid[name] = np.ascontiguousarray(value)
        if name in COL_NAMES:
            laid[f"{name}_col"] = np.ascontiguousarray(value.reshape(-1, P).T)
    nc = bacc.Bacc("TRN2", target_bir_lowering=False, num_devices=1)
    arrays, a = {}, {}
    for name, value in laid.items():
        arrays[f"in_{name}"] = value
        a[name] = nc.dram_tensor(f"in_{name}", value.shape, mybir.dt.from_np(value.dtype), kind="ExternalInput").ap()
    out = nc.dram_tensor("out_x", (B, S, D), F32, kind="ExternalOutput").ap()
    build(nc, a, out)
    r = run_bass_kernel_spmd(nc, [arrays], core_ids=[0])
    return r.results[0]["out_x"]
```
